# Optimizing a Trainium2 kernel written in Bass

```python
import numpy as np
import jax
import jax.numpy as jnp

def _softmax(x, axis=-1):
    return jax.nn.softmax(x, axis=axis)

def _gelu(x):
    return jax.nn.gelu(x, approximate=True)

def _silu(x):
    return jax.nn.silu(x)

def _sigmoid(x):
    return jax.nn.sigmoid(x)

def _layernorm(x, axis=-1, eps=1e-05):
    m = jnp.mean(x, axis=axis, keepdims=True)
    v = jnp.var(x, axis=axis, keepdims=True)
    return (x - m) / jnp.sqrt(v + eps)

def _scatter_add(tgt, idx, src, axis=0):
    return tgt.at[idx].add(src)

def _segment_sum(src, seg, n):
    return jax.ops.segment_sum(src, seg, n)
kernel_name = 'mk_sandwich_d1_jaxref_r2_cc0a2e'

def setup_inputs(seed: int=0):
    np.random.seed(seed)
    _w = jnp.asarray

    def _L0_attn_setup():
        import jax, jax.numpy as jnp
        import numpy as np
        B, S, D = (8, 1024, 512)
        key = jax.random.key(seed)
        x = jax.random.normal(key, (B, S, D), dtype=jnp.float32)
        return {'x': x}
    _L0_attn_in = _L0_attn_setup()

    def _L0_ffn_setup():
        import jax, jax.numpy as jnp
        import numpy as np
        NUM_EXPERTS = 8
        TOP_K = 2
        D_MODEL = 512
        EXPERT_CAP = 256
        B, S = (4, 1024)
        key = jax.random.key(seed)
        ks = jax.random.split(key, 4)
        scale = 1.0 / np.sqrt(D_MODEL)
        x = jax.random.normal(ks[0], (B, S, D_MODEL), dtype=jnp.float32)
        gate_w = jax.random.normal(ks[1], (D_MODEL, NUM_EXPERTS), dtype=jnp.float32) * scale
        w1 = jax.random.normal(ks[2], (NUM_EXPERTS, D_MODEL, EXPERT_CAP), dtype=jnp.float32) * scale
        b1 = jnp.zeros((NUM_EXPERTS, EXPERT_CAP), dtype=jnp.float32)
        w2 = jax.random.normal(ks[3], (NUM_EXPERTS, EXPERT_CAP, D_MODEL), dtype=jnp.float32) * (1.0 / np.sqrt(EXPERT_CAP))
        b2 = jnp.zeros((NUM_EXPERTS, D_MODEL), dtype=jnp.float32)
        return {'x': x, 'gate_w': gate_w, 'w1': w1, 'b1': b1, 'w2': w2, 'b2': b2}
    _L0_ffn_in = _L0_ffn_setup()
    _d = {'L0_attn_x': _L0_attn_in['x'], 'L0_ffn_gate_w': _L0_ffn_in['gate_w'], 'L0_ffn_w1': _L0_ffn_in['w1'], 'L0_ffn_b1': _L0_ffn_in['b1'], 'L0_ffn_w2': _L0_ffn_in['w2'], 'L0_ffn_b2': _L0_ffn_in['b2']}
    _x0 = _d['L0_attn_x']
    _d['L0_attn_x'] = jax.random.normal(jax.random.fold_in(jax.random.key(seed), 1), (8, 1024, 512), dtype=_x0.dtype)
    del _x0
    return _d

def reference(L0_attn_x, L0_ffn_gate_w, L0_ffn_w1, L0_ffn_b1, L0_ffn_w2, L0_ffn_b2):

    def _L0_attn_ref(x):
        import jax, jax.numpy as jnp
        import numpy as np
        B, S, D = (8, 1024, 512)
        scores = jnp.einsum('bid,bjd->bij', x, x)
        attn = jax.nn.softmax(scores, axis=1)
        context = jnp.einsum('bij,bjd->bid', attn, x)
        return context

    def _L0_ffn_ref(x, gate_w, w1, b1, w2, b2):
        import jax, jax.numpy as jnp
        import numpy as np
        NUM_EXPERTS = 8
        TOP_K = 2
        D_MODEL = 512
        EXPERT_CAP = 256
        B, S = (4, 1024)
        Bx, Sx, D = x.shape
        xt = x.reshape(-1, D)
        gates = jax.nn.softmax(xt @ gate_w, axis=-1)
        topk_g, topk_i = jax.lax.top_k(gates, TOP_K)
        tok_w = topk_g.sum(axis=-1)
        sel = (topk_i[:, :, None] == jnp.arange(NUM_EXPERTS)[None, None, :]).any(axis=1)
        h = jax.nn.gelu(jnp.einsum('nd,edh->enh', xt, w1) + b1[:, None, :], approximate=False)
        y = jnp.einsum('enh,ehd->end', h, w2) + b2[:, None, :]
        out = jnp.einsum('end,ne,n->nd', y, sel.astype(x.dtype), tok_w)
        return out.reshape(Bx, Sx, D)
    x = L0_attn_x
    x = x + _layernorm(_L0_attn_ref(_layernorm(x, axis=-1)), axis=-1)
    x = x + _layernorm(_L0_ffn_ref(_layernorm(x, axis=-1), L0_ffn_gate_w, L0_ffn_w1, L0_ffn_b1, L0_ffn_w2, L0_ffn_b2), axis=-1)
    return x

_drawn_inputs = setup_inputs


def setup_inputs(seed=0):
    import zlib

    import numpy as np

    out = dict(_drawn_inputs(seed))
    spreads = {'L0_ffn_b1': (0.0, 0.1), 'L0_ffn_b2': (0.0, 0.1)}
    factors = {}
    for name, (base, spread) in spreads.items():
        noise = np.random.default_rng([zlib.crc32(name.encode()), seed]).standard_normal(out[name].shape)
        drawn = base * np.exp(spread * noise) if base else spread * noise
        out[name] = jnp.asarray(drawn.astype(out[name].dtype))
    for name, factor in factors.items():
        out[name] = (out[name] * factor).astype(out[name].dtype)
    return out
```

```python
from contextlib import ExitStack

import numpy as np

import concourse.bass as bass
from concourse import mybir

F32 = mybir.dt.float32
F16 = mybir.dt.float16
U32 = mybir.dt.uint32
I32 = mybir.dt.int32
ALU = mybir.AluOpType
ACT = mybir.ActivationFunctionType
X = mybir.AxisListType.X

P = 128
SLOT = 256
EPS = 1e-5
PSCALE = 1024.0
WSCALE = 64.0
FAR = -1e30


def attention_then_experts(nc, x, gate_w, w1, b1, w2, b2, out):
    B, S, D = x.shape
    E, _, H = w1.shape
    T = S // P
    KD = D // P
    MH = H // P
    NTOK = B * S
    NT = B * T
    CAP = NTOK + SLOT
    G = 2 * NTOK // SLOT + E - 1
    ROW = D + 8
    HALF = 512
    assert T == 8 and KD == 4 and S == 2 * HALF and D == HALF and MH == 2 and G % 2 == 1 and B >= 3

    x_v = x.rearrange("b (t p) d -> b p t d", p=P)
    xt_v = x.rearrange("b (t p) d -> (b t) p d", p=P)
    out_v = out.rearrange("b (t p) d -> p (b t) d", p=P)
    lists = nc.dram_tensor("slot_lists", (E * CAP + (E - 1) * SLOT, ROW), F32, kind="Internal").ap()
    acc = nc.dram_tensor("expert_sum", (NTOK + SLOT, D), F32, kind="Internal").ap()
    mid = nc.dram_tensor("after_attention", (NTOK, D), F32, kind="Internal").ap()
    mid_t = mid.rearrange("(n p) d -> n p d", p=P)
    mid_v = mid.rearrange("(n p) d -> p n d", p=P)
    acc_t = acc.rearrange("(n p) d -> n p d", p=P)
    acc_v = acc.rearrange("(n p) d -> p n d", p=P)

    with ExitStack() as ctx:
        def sem(name):
            return ctx.enter_context(nc.semaphore(name))

        def sb(name, shape, dt, where=ctx):
            return where.enter_context(nc.sbuf_tensor(name, shape, dt))

        def bank(name, where=ctx, shape=(P, HALF)):
            return where.enter_context(nc.psum_tensor(name, list(shape), F32))

        ident = sb("ident", [P, P], F32)
        before = sb("before", [P, P], F16)
        ones = sb("ones", [P, P], F16)
        pow_exp = sb("pow_exp", [P, T], F32)
        rev = sb("rev", [P, E], F32)
        gate = sb("gate", [P, KD, E], F32)
        b1_col = sb("b1_col", [P, E * MH], F32)
        tok_w = sb("tok_w", [P, NT], F32)
        z = sb("z", [P, T, ROW], F32)
        pad = sb("pad", [P, 2, ROW], F32)
        token = sb("token", [P, T], F32)
        carry = sb("carry", [P, E], F32)
        ctxn = sb("ctxn", [P, 2, D], F32)
        xres = sb("xres", [P, 2, D], F32)
        x1 = sb("x1", [P, 2, D], F32)
        zT = sb("zT", [P, D], F32)
        lgT = sb("lgT", [E, S], F32)
        lg = sb("lg", [P, T, E], F32)
        lg2 = sb("lg2", [P, T, E], F32)
        lgd = sb("lgd", [P, T, E], F32)
        lge = sb("lge", [P, T, E], F32)
        eq = sb("eq", [P, T, E], F32)
        first = sb("first", [P, T, E], F32)
        second = sb("second", [P, T, E], F32)
        chosen = sb("chosen", [P, T, E], F16)
        gnum = sb("gnum", [P, T, E], F32)
        place = sb("place", [P, T, E], F32)
        place1 = sb("place1", [P, T, E], F32)
        place2 = sb("place2", [P, T, E], F32)
        top = sb("top", [P, 6, T], F32)
        slot_f = sb("slot_f", [P, T, 2], F32)
        slot = sb("slot", [P, T, 2], U32)
        pad_f = sb("pad_f", [P, E, 2], F32)
        pad_at = sb("pad_at", [P, E, 2], U32)
        lane = sb("lane", [P, 2], F32)
        st_x = sb("st_x", [P, T, 6], F32)
        mv_x = sb("mv_x", [P, T, 2], F32)
        var_x = sb("var_x", [P, T], F32)
        rstd_x = sb("rstd_x", [P, T], F32)
        off_x = sb("off_x", [P, T], F32)
        st_c = sb("st_c", [P, T, 6], F32)
        mv_c = sb("mv_c", [P, T, 2], F32)
        var_c = sb("var_c", [P, T], F32)
        rstd_c = sb("rstd_c", [P, T], F32)
        off_c = sb("off_c", [P, T], F32)
        st_z = sb("st_z", [P, T, 6], F32)
        mv_z = sb("mv_z", [P, T, 2], F32)
        var_z = sb("var_z", [P, T], F32)
        rstd_z = sb("rstd_z", [P, T], F32)
        off_z = sb("off_z", [P, T], F32)
        neg_max = sb("neg_max", [P, T], F32)
        psum_row = sb("psum_row", [P, T], F32)
        psum_sc = sb("psum_sc", [P, T], F32)
        pinv = sb("pinv", [P, T], F32)
        tab = {n: sb(f"tab_{n}", [1, w], F32) for n, w in
               (("cnt", E), ("tiles", E), ("ones", E), ("end", E), ("g", G))}
        tab_big = sb("tab_big", [1, G, E], F32)
        tab_big2 = sb("tab_big2", [1, G, E], F32)
        tab_e = sb("tab_e", [1, G], F32)
        tab_k = sb("tab_k", [1, G], F32)
        tab_c = sb("tab_c", [1, G], F32)
        tab_r = sb("tab_r", [1, G], F32)
        tab_i = sb("tab_i", [1, E], I32)
        tab_i2 = sb("tab_i2", [1, E], I32)
        tile_row = sb("tile_row", [1, G], I32)
        tile_e = sb("tile_e", [1, G], I32)

        with ExitStack() as a:
            y = sb("y", [P, T, D], F32, a)
            y_hi = sb("y_hi", [P, T, D], F16, a)
            y_lo = sb("y_lo", [P, T, D], F16, a)
            yT_hi = sb("yT_hi", [P, KD, S], F16, a)
            yT_lo = sb("yT_lo", [P, KD, S], F16, a)
            p_hi = sb("p_hi", [P, T, S], F16, a)
            p_lo = sb("p_lo", [P, T, S], F16, a)
            p32 = sb("p32", [P, 3, S], F32, a)
            above = [sb(f"above{j}", [P, S - P * (j + 1)], F32, a) for j in range(T - 1)]
        with ExitStack() as a:
            stage = sb("stage", [P, 4, KD * H], F32, a)
            w1_hi = sb("w1_hi", [P, E, KD * H], F16, a)
            w1_lo = sb("w1_lo", [P, E, KD * H], F16, a)
            w2_hi = sb("w2_hi", [P, E, MH * D], F16, a)
            w2_lo = sb("w2_lo", [P, E, MH * D], F16, a)
            b2_all = sb("b2_all", [P, E * D], F32, a)
            zin = sb("zin", [P, 2, 2, ROW], F32, a)
            s_hi = sb("s_hi", [P, 2, KD * SLOT], F16, a)
            s_lo = sb("s_lo", [P, 2, KD * SLOT], F16, a)
            h32 = sb("h32", [P, 2, MH * SLOT], F32, a)
            h_hi = sb("h_hi", [P, 2, MH * SLOT], F16, a)
            h_lo = sb("h_lo", [P, 2, MH * SLOT], F16, a)
            yo = sb("yo", [P, 2, 2, D], F32, a)
            who_all = sb("who_all", [P, 2 * G], U32, a)
            who = sb("who", [P, 2, 2], U32, a)
        with ExitStack() as a:
            QT = 4
            fin_a = sb("fin_a", [P, 2, QT, D], F32, a)
            fin_x = sb("fin_x", [P, 2, QT, D], F32, a)
            st_f = sb("st_f", [P, 2, QT, 6], F32, a)
            mv_f = sb("mv_f", [P, 2, QT, 2], F32, a)
            w_sq = sb("w_sq", [P, 2, QT], F32, a)
            var_f = sb("var_f", [P, 2, QT], F32, a)
            ve_f = sb("ve_f", [P, 2, QT], F32, a)
            rstd_f = sb("rstd_f", [P, 2, QT], F32, a)
            mul_f = sb("mul_f", [P, 2, QT], F32, a)
            off_f = sb("off_f", [P, 2, QT], F32, a)

        with ExitStack() as a:
            s_ps = [bank(f"s_ps{i}", a, (P, S)) for i in range(2)]
            c_ps = [bank(f"c_ps{i}", a) for i in range(2)]
            t_ps = bank("t_ps", a)
            z_ps = bank("z_ps", a)
        with ExitStack() as a:
            tr_ps = [bank(f"tr_ps{i}", a) for i in range(2)]
            h_ps = [bank(f"h_ps{i}", a) for i in range(2)]
            y_ps = [[bank(f"y_ps{i}{s}", a) for s in range(2)] for i in range(2)]

        consts = sem("consts")
        dve_consts = sem("dve_consts")
        const_dma = sem("const_dma")
        x_in = sem("x_in")
        xres_in = [sem(f"xres_in{i}") for i in range(2)]
        mid_out = [sem(f"mid_out{i}") for i in range(2)]
        zero_out = sem("zero_out")
        ln1_stats, ln1_mv, ln1_var, ln1_rstd, ln1_off = (sem(f"ln1_{n}") for n in ("stats", "mv", "var", "rstd", "off"))
        y_done = sem("y_done")
        yT_done, yT_hi_done, yT_lo_done = sem("yT_done"), sem("yT_hi_done"), sem("yT_lo_done")
        yhi_done, ylo_done = sem("yhi_done"), sem("ylo_done")
        s_done, above_done, exp_done = sem("s_done"), sem("above_done"), sem("exp_done")
        max_done, sum_done, inv_done = sem("max_done"), sem("sum_done"), sem("inv_done")
        phi_done, plo_done, pv_done = sem("phi_done"), sem("plo_done"), sem("pv_done")
        c_stats, c_mv, c_var, c_rstd, c_off = (sem(f"c_{n}") for n in ("stats", "mv", "var", "rstd", "off"))
        z_stats, z_mv, z_var, z_rstd, z_off = (sem(f"z_{n}") for n in ("stats", "mv", "var", "rstd", "off"))
        ctxn_done, x1_done, z_done = sem("ctxn_done"), sem("x1_done"), sem("z_done")
        ztr_done, zT_done, gate_done, lgT_done = sem("ztr_done"), sem("zT_done"), sem("gate_done"), sem("lgT_done")
        lg_ready, lgd_done, lge_done = sem("lg_ready"), sem("lgd_done"), sem("lge_done")
        route, chosen_done, rank_done, slot_done = sem("route"), sem("chosen_done"), sem("rank_done"), sem("slot_done")
        scat = [sem(f"scat{t}") for t in range(T)]
        slot_f_done = sem("slot_f_done")
        pads_at, pads_out, tab_step, tab_done = sem("pads_at"), sem("pads_out"), sem("tab_step"), sem("tab_done")
        w_in = [sem(f"w_in{i}") for i in range(4)]
        whi_done, wlo_done, b_in = sem("whi_done"), sem("wlo_done"), sem("b_in")
        zin_in = [sem(f"zin_in{i}") for i in range(2)]
        tr_done, shi_done, slo_done = sem("tr_done"), sem("shi_done"), sem("slo_done")
        who_in, who_done = sem("who_in"), sem("who_done")
        h_done, gelu_done, hhi_done, hlo_done = sem("h_done"), sem("gelu_done"), sem("hhi_done"), sem("hlo_done")
        ye_done, yo_done = sem("ye_done"), sem("yo_done")
        added = sem("added")
        fin_in = [sem(f"fin_in{i}") for i in range(2)]
        f_stats, f_mv, f_sq, f_var, f_ve, f_rstd, f_mul, f_off = (
            sem(f"f_{n}") for n in ("stats", "mv", "sq", "var", "ve", "rstd", "mul", "off"))
        f_norm, f_sum = sem("f_norm"), sem("f_sum")
        fin_out = [sem(f"fin_out{i}") for i in range(2)]

        NCONST = 12
        ROUTE = 20
        TAB = 9
        SH = SLOT // P
        STAGES = 2 * E
        NF = NT // QT

        def batches(eng, one):
            one(0, False)
            with eng.Fori(1, B - 1) as b:
                one(b, True)
            one(B - 1, True)

        def expert_steps(eng, one):
            for s in range(3):
                one(s)
            with eng.Fori(0, (G - 5) // 2) as i:
                one(2 * i + 3, 1)
                one(2 * i + 4, 0)
            for s in range(G - 2, G + 1):
                one(s)

        block = ctx.enter_context(nc.Block())

        @block.sync
        def _(sp):
            sp.dma_start(y[:, :, :], x_v[0]).then_inc(x_in, 16)
            sp.dma_start(gate[:, :, :], gate_w.rearrange("(k p) e -> p k e", p=P)).then_inc(const_dma, 16)
            sp.dma_start(b1_col[:, :], b1.rearrange("e (m p) -> p (e m)", p=P),
                         allow_slow_non_contiguous=True).then_inc(b_in, 16)
            for i in range(2):
                sp.dma_start(xres[:, i, :], xt_v[i]).then_inc(xres_in[i], 16)
            sp.wait_ge(consts, NCONST)
            for n in range(NTOK // P + SH):
                sp.dma_start(acc_t[n], pad[:, 0, 0:D]).then_inc(zero_out, 16)
            for n in range(E - 1):
                at = E * CAP + n * SLOT
                sp.dma_start(lists[at:at + SLOT, :].rearrange("(s p) r -> p s r", p=P),
                             pad[:, :, :]).then_inc(zero_out, 16)

            def batch(b, tail):
                last = isinstance(b, int) and b == B - 1
                if not last:
                    sp.wait_ge(ylo_done, T * (b + 1))
                    sp.dma_start(y[:, :, :], x_v[bass.ds(b + 1, 1)].rearrange("b p t d -> p (b t) d")
                                 ).then_inc(x_in, 16)
                for t in range(T):
                    m = T * b + t
                    sp.wait_ge(x1_done, m + 1)
                    sp.dma_start(mid_t[bass.ds(m, 1)].rearrange("n p d -> p (n d)"),
                                 x1[:, t % 2, :]).then_inc(mid_out[t % 2], 16)
                    if not (last and t >= T - 2):
                        sp.dma_start(xres[:, t % 2, :], xt_v[bass.ds(m + 2, 1)].rearrange("n p d -> p (n d)")
                                     ).then_inc(xres_in[t % 2], 16)
            batches(sp, batch)

            sp.wait_ge(pv_done, NT)
            sp.wait_ge(ctxn_done, NT)
            sp.dma_start(b2_all[:, :], b2.rearrange("e d -> (e d)").partition_broadcast(P)).then_inc(b_in, 16)
            for i in range(STAGES):
                if i >= 4:
                    sp.wait_ge(wlo_done, i - 3)
                e, second_w = i // 2, i % 2
                src = (w2[e].rearrange("(m p) d -> p m d", p=P) if second_w
                       else w1[e].rearrange("(k p) h -> p k h", p=P))
                sp.dma_start(stage[:, i % 4, :].rearrange("p (k h) -> p k h", k=MH if second_w else KD),
                             src).then_inc(w_in[i % 4], 16)

            for t in range(T):
                sp.wait_ge(scat[t], 32 * B)
            sp.wait_ge(pads_out, 16 * 2 * E)
            sp.wait_ge(zero_out, 16 * (NTOK // P + SH + E - 1))
            sp.wait_ge(tab_done, 1)

            def load_slots(g, par):
                if not isinstance(g, int) or g >= 2:
                    sp.wait_ge(tr_done, 2 * (g - 1))
                    sp.wait_ge(who_in, g - 1)
                row = sp.value_load(tile_row[0:1, bass.ds(g, 1)], min_val=0,
                                    max_val=E * CAP + (E - 2) * SLOT)
                sp.dma_start(zin[:, par, :, :], lists[bass.ds(row, SLOT), :].rearrange("(s p) r -> p s r", p=P)
                             ).then_inc(zin_in[par], 16)
            load_slots(0, 0)
            load_slots(1, 1)
            with sp.Fori(0, (G - 3) // 2) as i:
                load_slots(2 * i + 2, 0)
                load_slots(2 * i + 3, 1)
            load_slots(G - 1, 0)

            sp.wait_ge(added, 16 * SH * G)
            for i in range(2):
                sp.wait_ge(mid_out[i], 16 * NT // 2)
            sp.wait_ge(ye_done, SH * G)

            def load_final(q, par):
                n = QT * q
                if not isinstance(q, int) or q >= 2:
                    sp.wait_ge(fin_out[par], 16 * (q // 2) if isinstance(q, int) else 8 * (q - par))
                    sp.wait_ge(f_sum, q - 1)
                sp.dma_start(fin_a[:, par, :, :], acc_v[:, bass.ds(n, QT), :]).then_inc(fin_in[par], 16)
                sp.dma_start(fin_x[:, par, :, :], mid_v[:, bass.ds(n, QT), :]).then_inc(fin_in[par], 16)
            load_final(0, 0)
            load_final(1, 1)

            def store_final(q, par):
                sp.wait_ge(f_sum, q + 1)
                sp.dma_start(out_v[:, bass.ds(QT * q, QT), :], fin_x[:, par, :, :]).then_inc(fin_out[par], 16)
            with sp.Fori(0, NF // 2 - 1) as i:
                store_final(2 * i, 0)
                load_final(2 * i + 2, 0)
                store_final(2 * i + 1, 1)
                load_final(2 * i + 3, 1)
            store_final(NF - 2, 0)
            store_final(NF - 1, 1)
            for i in range(2):
                sp.wait_ge(fin_out[i], 16 * NF // 2)

        @block.gpsimd
        def _(pool):
            pool.memset(ident[:, :], 0.0).then_inc(consts, 1)
            pool.memset(before[:, :], 1.0).then_inc(consts, 1)
            pool.memset(pow_exp[:, :], -0.5).then_inc(consts, 1)
            pool.memset(z[:, :, :], 0.0).then_inc(consts, 1)
            pool.memset(pad[:, :, :], 0.0).then_inc(consts, 1)
            pool.wait_ge(consts, 5)
            pool.affine_select(out=ident[:, :], in_=ident[:, :], compare_op=ALU.not_equal, fill=1.0,
                               base=0, pattern=[[-1, P]], channel_multiplier=1).then_inc(consts, 1)
            pool.affine_select(out=before[:, :], in_=before[:, :], compare_op=ALU.is_gt, fill=0.0,
                               base=0, pattern=[[1, P]], channel_multiplier=-1).then_inc(consts, 1)
            pool.iota(token[:, :], pattern=[[P, T]], base=-S, channel_multiplier=1,
                      allow_small_or_imprecise_dtypes=True).then_inc(consts, 1)
            pool.iota(lane[:, :], pattern=[[P, 2]], base=0, channel_multiplier=1,
                      allow_small_or_imprecise_dtypes=True).then_inc(consts, 1)
            pool.iota(carry[:, :], pattern=[[CAP, E]], base=0, channel_multiplier=0,
                      allow_small_or_imprecise_dtypes=True).then_inc(consts, 1)
            pool.iota(rev[:, :], pattern=[[-1, E]], base=E, channel_multiplier=0,
                      allow_small_or_imprecise_dtypes=True).then_inc(consts, 1)
            pool.iota(pad[:, :, D:D + 1].bitcast(U32).rearrange("p s r -> p (s r)"), pattern=[[P, 2]], base=NTOK,
                      channel_multiplier=1).then_inc(consts, 1)
            pool.iota(tab["g"][:, :], pattern=[[1, G]], base=0, channel_multiplier=0,
                      allow_small_or_imprecise_dtypes=True).then_inc(tab_step, 1)

            def power(out, in_, wait, n, done):
                pool.wait_ge(wait, n)
                pool.tensor_tensor(out, in_, pow_exp[:, 0:in_.shape[1]], ALU.pow).then_inc(done, 1)

            def scatter(q, t):
                pool.wait_ge(slot_done, q + 1)
                pool.nop(nofuse=True)
                for k in range(2):
                    pool.indirect_dma_start(out=lists, in_=z[:, t, :], in_offset=None,
                                            out_offset=bass.IndirectOffsetOnAxis(ap=slot[:, t, k:k + 1], axis=0)
                                            ).then_inc(scat[t], 16)

            def batch(b, has_tail):
                last = isinstance(b, int) and b == B - 1
                for j in range(T):
                    if has_tail:
                        pool.wait_ge(pv_done, T * b)
                    pool.wait_ge(yhi_done, T * b + j + 1)
                    pool.tensor_tensor(y_lo[:, j, :], y[:, j, :], y_hi[:, j, :], ALU.subtract).then_inc(ylo_done, 1)
                if not last:
                    power(rstd_x[:, :], var_x[:, :], ln1_var, b + 2, ln1_rstd)
                for t in range(T):
                    m = T * b + t
                    power(rstd_c[:, t:t + 1], var_c[:, t:t + 1], c_var, m + 1, c_rstd)
                    if t:
                        power(rstd_z[:, t - 1:t], var_z[:, t - 1:t], z_var, m, z_rstd)
                    pool.wait_ge(ctxn_done, m + 1)
                    half_batch = T // 2
                    pool.wait_ge(xres_in[t % 2], 16 * (half_batch * b + t // 2 + 1))
                    if t >= 2 or has_tail:
                        pool.wait_ge(mid_out[t % 2], 16 * (half_batch * b + t // 2))
                        pool.wait_ge(z_done, m - 1)
                    pool.tensor_tensor(x1[:, t % 2, :], xres[:, t % 2, :], ctxn[:, t % 2, :], ALU.add).then_inc(x1_done, 1)
                    if has_tail:
                        scatter(b - 1, t)
                power(rstd_z[:, T - 1:T], var_z[:, T - 1:T], z_var, T * b + T, z_rstd)

            power(rstd_x[:, :], var_x[:, :], ln1_var, 1, ln1_rstd)
            batches(pool, batch)
            for t in range(T):
                scatter(B - 1, t)
            pool.wait_ge(pads_at, 1)
            for e in range(E):
                for s in range(SH):
                    pool.indirect_dma_start(out=lists, in_=pad[:, s, :], in_offset=None,
                                            out_offset=bass.IndirectOffsetOnAxis(ap=pad_at[:, e, s:s + 1], axis=0)
                                            ).then_inc(pads_out, 16)

            def add_rows(g, par):
                pool.wait_ge(who_done, g + 1)
                for s in range(SH):
                    pool.wait_ge(yo_done, SH * g + s + 1)
                    if not isinstance(g, int) or g or s:
                        pool.wait_ge(added, 16 * (SH * g + s))
                    pool.nop(nofuse=True)
                    pool.indirect_dma_start(out=acc, in_=yo[:, par, s, :], in_offset=None, compute_op=ALU.add,
                                            out_offset=bass.IndirectOffsetOnAxis(ap=who[:, par, s:s + 1], axis=0)
                                            ).then_inc(added, 16)
            pool.wait_ge(zero_out, 16 * (NTOK // P + SH + E - 1))
            add_rows(0, 0)
            with pool.Fori(0, (G - 3) // 2) as i:
                add_rows(2 * i + 1, 1)
                add_rows(2 * i + 2, 0)
            add_rows(G - 2, 1)
            add_rows(G - 1, 0)

            def final(q, par):
                pool.wait_ge(f_ve, q + 1)
                pool.tensor_tensor(rstd_f[:, par, :], ve_f[:, par, :], pow_exp[:, 0:QT], ALU.pow).then_inc(f_rstd, 1)
                pool.wait_ge(f_norm, QT * (q + 1))
                pool.tensor_tensor(fin_x[:, par, :, :], fin_x[:, par, :, :], fin_a[:, par, :, :], ALU.add).then_inc(f_sum, 1)
            with pool.Fori(0, NF // 2) as i:
                final(2 * i, 0)
                final(2 * i + 1, 1)

        @block.scalar
        def _(act):
            def norm_x(q, t):
                act.wait_ge(ln1_off, q + 1)
                act.activation(y[:, t, :], y[:, t, :], ACT.Identity, bias=off_x[:, t:t + 1],
                               scale=rstd_x[:, t:t + 1]).then_inc(y_done, 1)

            def yT_high(q, t):
                act.wait_ge(yT_done, T * q + t + 1)
                act.activation(yT_hi[:, :, t * P:(t + 1) * P], t_ps[:, :].rearrange("p (k c) -> p k c", k=KD),
                               ACT.Copy).then_inc(yT_hi_done, 1)

            def norm_z(q, t, guard):
                act.wait_ge(z_off, T * q + t + 1)
                if guard:
                    act.wait_ge(scat[t], 32 * q)
                act.activation(z[:, t, 0:D], x1[:, t % 2, :], ACT.Identity, bias=off_z[:, t:t + 1],
                               scale=rstd_z[:, t:t + 1]).then_inc(z_done, 1)

            def copy_zT(q, t):
                act.wait_ge(ztr_done, T * q + t + 1)
                act.activation(zT[:, :], z_ps[:, :], ACT.Copy).then_inc(zT_done, 1)

            def copy_lgT(q, t):
                act.wait_ge(gate_done, T * q + t + 1)
                act.activation(lgT[:, t * P:(t + 1) * P], z_ps[0:E, 0:P], ACT.Copy).then_inc(lgT_done, 1)

            def p_high(b, j):
                act.wait_ge(inv_done, T * b + j + 1)
                act.activation(p_hi[:, j, :], p32[:, j % 3, :], ACT.Copy, scale=pinv[:, j:j + 1]).then_inc(phi_done, 1)

            def tail(q, j):
                if j == 0:
                    copy_lgT(q, T - 3)
                    copy_zT(q, T - 2)
                if j == 1:
                    copy_lgT(q, T - 2)
                    copy_zT(q, T - 1)
                if j == 2:
                    copy_lgT(q, T - 1)
                if j == 4:
                    act.wait_ge(lgd_done, q + 1)
                    act.activation(lge[:, :, :], lgd[:, :, :], ACT.Exp).then_inc(lge_done, 1)

            def batch(b, has_tail):
                last = isinstance(b, int) and b == B - 1
                for j in range(T):
                    n = T * b + j
                    if has_tail:
                        act.wait_ge(pv_done, T * b)
                    act.wait_ge(y_done, n + 1)
                    act.activation(y_hi[:, j, :], y[:, j, :], ACT.Copy).then_inc(yhi_done, 1)
                    act.wait_ge(max_done, n + 1)
                    sp_ = s_ps[j % 2]
                    if j < T - 1:
                        act.activation(above[j][:, :], sp_[:, (j + 1) * P:S], ACT.Copy).then_inc(above_done, 1)
                    if j >= 3:
                        act.wait_ge(plo_done, n - 2)
                    act.activation(p32[:, j % 3, :], sp_[:, :], ACT.Exp, bias=neg_max[:, j:j + 1],
                                   accum_out=psum_row[:, j:j + 1]).then_inc(exp_done, 1)
                    if j:
                        p_high(b, j - 1)
                    if has_tail:
                        tail(b - 1, j)
                p_high(b, T - 1)
                if not last:
                    norm_x(b + 1, 0)
                    norm_x(b + 1, 1)
                for t in range(T):
                    m = T * b + t
                    if t >= 3:
                        copy_lgT(b, t - 3)
                    if t >= 1 and not last:
                        yT_high(b + 1, t - 1)
                    if t >= 2:
                        copy_zT(b, t - 2)
                    act.wait_ge(c_off, m + 1)
                    act.activation(ctxn[:, t % 2, :], c_ps[t % 2][:, :], ACT.Identity, bias=off_c[:, t:t + 1],
                                   scale=rstd_c[:, t:t + 1]).then_inc(ctxn_done, 1)
                    if t >= 1:
                        norm_z(b, t - 1, has_tail)
                    if t + 2 < T and not last:
                        norm_x(b + 1, t + 2)
                if not last:
                    yT_high(b + 1, T - 1)
                norm_z(b, T - 1, has_tail)

            for t in range(T):
                norm_x(0, t)
            for t in range(T):
                yT_high(0, t)
            batches(act, batch)
            for j in range(T):
                tail(B - 1, j)

            for i in range(STAGES):
                e, dst = i // 2, (w2_hi if i % 2 else w1_hi)
                act.wait_ge(w_in[i % 4], 16 * (i // 4 + 1))
                act.activation(dst[:, e, :], stage[:, i % 4, :], ACT.Copy, scale=WSCALE).then_inc(whi_done, 1)
            act.wait_ge(b_in, 32)
            act.wait_ge(tab_done, 1)

            def slots_high(g, par):
                for c in range(2):
                    act.wait_ge(tr_done, 2 * g + c + 1)
                    if c == 0 and (not isinstance(g, int) or g >= 2):
                        act.wait_ge(h_done, g - 1)
                    act.activation(s_hi[:, par, c * HALF:(c + 1) * HALF], tr_ps[c][:, :], ACT.Copy).then_inc(shi_done, 1)

            def gelu(g, par):
                e2 = act.value_load(tile_e[0:1, bass.ds(g, 1)], min_val=0, max_val=E - 1) * MH
                act.wait_ge(h_done, g + 1)
                if not isinstance(g, int) or g >= 2:
                    act.wait_ge(hlo_done, g - 1)
                for m in range(MH):
                    act.activation(h32[:, par, m * SLOT:(m + 1) * SLOT], h_ps[par][:, m * SLOT:(m + 1) * SLOT],
                                   ACT.Gelu, bias=b1_col[:, bass.ds(e2 + m, 1)], scale=1.0 / WSCALE).then_inc(gelu_done, 1)

            def step(s, par=None):
                par = s % 2 if par is None else par
                if not isinstance(s, int) or s + 1 < G:
                    slots_high(s + 1, 1 - par)
                if not isinstance(s, int) or s < G:
                    gelu(s, par)
            slots_high(0, 0)
            expert_steps(act, step)

            def final(q, par):
                act.wait_ge(f_off, q + 1)
                for t in range(QT):
                    act.activation(fin_a[:, par, t, :], fin_a[:, par, t, :], ACT.Identity, bias=off_f[:, par, t:t + 1],
                                   scale=mul_f[:, par, t:t + 1]).then_inc(f_norm, 1)
            with act.Fori(0, NF // 2) as i:
                final(2 * i, 0)
                final(2 * i + 1, 1)

        @block.vector
        def _(dve):
            dve.memset(ones[:, :], 1.0).then_inc(dve_consts, 1)
            dve.memset(tab["ones"][:, :], 1.0).then_inc(dve_consts, 1)

            def stats(src, st, mv, var, off, rstd, eps, done, i, n):
                stat_s, mv_s, var_s = done
                dve.bn_stats(st[:, i, :], src).then_inc(stat_s, 1)
                dve.wait_ge(stat_s, n + 1)
                dve.nop(nofuse=True)
                dve.bn_aggr(mv[:, i, :], st[:, i, :]).then_inc(mv_s, 1)
                dve.wait_ge(mv_s, n + 1)
                dve.tensor_scalar(var[:, i:i + 1], mv[:, i, 1:2], eps, None, ALU.add).then_inc(var_s, 1)

            def offset(mv, rstd, off, rstd_s, off_s, i, n):
                dve.wait_ge(rstd_s, n + 1)
                dve.scalar_tensor_tensor(off[:, i:i + 1], mv[:, i, 0:1], -1.0, rstd[:, i:i + 1],
                                         ALU.mult, ALU.mult).then_inc(off_s, 1)

            def ln1(q):
                dve.wait_ge(x_in, 16 * (q + 1))
                for t in range(T):
                    last = dve.bn_stats(st_x[:, t, :], y[:, t, :])
                last.then_inc(ln1_stats, 1)
                dve.wait_ge(ln1_stats, q + 1)
                dve.nop(nofuse=True)
                for t in range(T):
                    last = dve.bn_aggr(mv_x[:, t, :], st_x[:, t, :])
                last.then_inc(ln1_mv, 1)
                dve.wait_ge(ln1_mv, q + 1)
                dve.tensor_scalar(var_x[:, :], mv_x[:, :, 1], EPS, None, ALU.add).then_inc(ln1_var, 1)
                dve.wait_ge(ln1_rstd, q + 1)
                dve.scalar_tensor_tensor(off_x[:, :], mv_x[:, :, 0], -1.0, rstd_x[:, :], ALU.mult, ALU.mult).then_inc(ln1_off, 1)

            def yT_low(q, t):
                dve.wait_ge(yT_hi_done, T * q + t + 1)
                cols = slice(t * P, (t + 1) * P)
                dve.tensor_tensor(yT_lo[:, :, cols], t_ps[:, :].rearrange("p (k c) -> p k c", k=KD),
                                  yT_hi[:, :, cols], ALU.subtract).then_inc(yT_lo_done, 1)

            def c_step(m, t):
                dve.wait_ge(pv_done, m + 1)
                stats(c_ps[t % 2][:, :], st_c, mv_c, var_c, off_c, rstd_c, EPS * PSCALE * PSCALE,
                      (c_stats, c_mv, c_var), t, m)

            def z_step(m, t):
                dve.wait_ge(x1_done, m + 1)
                stats(x1[:, t % 2, :], st_z, mv_z, var_z, off_z, rstd_z, EPS, (z_stats, z_mv, z_var), t, m)

            def row_sum(b, j):
                n = T * b + j
                dve.wait_ge(exp_done, n + 1)
                dve.tensor_scalar(psum_sc[:, j:j + 1], psum_row[:, j:j + 1], 1.0 / PSCALE, None, ALU.mult).then_inc(sum_done, 1)
                dve.wait_ge(sum_done, n + 1)
                dve.reciprocal(pinv[:, j:j + 1], psum_sc[:, j:j + 1]).then_inc(inv_done, 1)

            def p_low(b, j):
                dve.wait_ge(phi_done, T * b + j + 1)
                dve.scalar_tensor_tensor(p_lo[:, j, :], p32[:, j % 3, :], pinv[:, j:j + 1], p_hi[:, j, :],
                                         ALU.mult, ALU.subtract).then_inc(plo_done, 1)

            def wide(col):
                return col.unsqueeze(2).broadcast_to([P, T, E])

            def across(row):
                return row.unsqueeze(1).broadcast_to([P, T, E])

            def router(q, part):
                base = ROUTE * q
                flat = "p t e -> p (t e)"
                if part == 0:
                    dve.wait_ge(lg_ready, q + 1)
                    dve.tensor_copy(lg[:, :, :].rearrange(flat), z_ps[:, 0:T * E]).then_inc(route, 1)
                    dve.wait_ge(route, base + 1)
                    dve.tensor_reduce(top[:, 0, :], lg[:, :, :], X, ALU.max).then_inc(route, 1)
                    dve.wait_ge(route, base + 2)
                    dve.tensor_tensor(lgd[:, :, :], lg[:, :, :], wide(top[:, 0, :]), ALU.subtract).then_inc(lgd_done, 1)
                    dve.tensor_tensor(eq[:, :, :], lg[:, :, :], wide(top[:, 0, :]), ALU.is_equal).then_inc(route, 1)
                    dve.wait_ge(route, base + 3)
                    dve.tensor_tensor(gnum[:, :, :], eq[:, :, :], across(rev[:, :]), ALU.mult).then_inc(route, 1)
                    dve.wait_ge(route, base + 4)
                    dve.tensor_reduce(top[:, 1, :], gnum[:, :, :], X, ALU.max).then_inc(route, 1)
                    dve.wait_ge(route, base + 5)
                    dve.tensor_tensor(first[:, :, :], across(rev[:, :]), wide(top[:, 1, :]), ALU.is_equal).then_inc(route, 1)
                    dve.wait_ge(route, base + 6)
                    dve.scalar_tensor_tensor(lg2[:, :, :].rearrange(flat), first[:, :, :].rearrange(flat), FAR,
                                             lg[:, :, :].rearrange(flat), ALU.mult, ALU.add).then_inc(route, 1)
                    dve.wait_ge(route, base + 7)
                    dve.tensor_reduce(top[:, 2, :], lg2[:, :, :], X, ALU.max).then_inc(route, 1)
                    dve.wait_ge(route, base + 8)
                    dve.tensor_tensor(eq[:, :, :], lg2[:, :, :], wide(top[:, 2, :]), ALU.is_equal).then_inc(route, 1)
                    dve.wait_ge(route, base + 9)
                    dve.tensor_tensor(gnum[:, :, :], eq[:, :, :], across(rev[:, :]), ALU.mult).then_inc(route, 1)
                    dve.wait_ge(route, base + 10)
                    dve.tensor_reduce(top[:, 3, :], gnum[:, :, :], X, ALU.max).then_inc(route, 1)
                    dve.wait_ge(route, base + 11)
                    dve.tensor_tensor(second[:, :, :], across(rev[:, :]), wide(top[:, 3, :]), ALU.is_equal).then_inc(route, 1)
                    dve.wait_ge(route, base + 12)
                    dve.tensor_tensor(chosen[:, :, :], first[:, :, :], second[:, :, :], ALU.add).then_inc(chosen_done, 1)
                if part == 1:
                    dve.wait_ge(lge_done, q + 1)
                    dve.wait_ge(chosen_done, q + 1)
                    dve.tensor_tensor(gnum[:, :, :], chosen[:, :, :], lge[:, :, :], ALU.mult).then_inc(route, 1)
                    dve.tensor_reduce(top[:, 4, :], lge[:, :, :], X, ALU.add).then_inc(route, 1)
                    dve.wait_ge(route, base + 14)
                    dve.tensor_reduce(top[:, 5, :], gnum[:, :, :], X, ALU.add).then_inc(route, 1)
                    dve.reciprocal(top[:, 0, :], top[:, 4, :]).then_inc(route, 1)
                    dve.wait_ge(route, base + 16)
                    dve.tensor_tensor(tok_w[:, bass.ds(T * q, T)], top[:, 5, :], top[:, 0, :], ALU.mult).then_inc(route, 1)
                if part == 2:
                    dve.wait_ge(rank_done, q + 1)
                    dve.tensor_tensor(place[:, :, :], z_ps[:, T * E:2 * T * E].rearrange("p (t e) -> p t e", e=E),
                                      across(carry[:, :]), ALU.add).then_inc(route, 1)
                    dve.wait_ge(route, base + 18)
                    dve.tensor_tensor(carry[:, :], carry[:, :], z_ps[:, 2 * T * E:2 * T * E + E], ALU.add).then_inc(route, 1)
                    dve.tensor_tensor(place1[:, :, :], place[:, :, :], first[:, :, :], ALU.mult)
                    dve.tensor_tensor(place2[:, :, :], place[:, :, :], second[:, :, :], ALU.mult)
                    dve.tensor_scalar(token[:, :], token[:, :], float(S), None, ALU.add).then_inc(route, 1)
                    dve.wait_ge(route, base + 20)
                    dve.tensor_reduce(slot_f[:, :, 0], place1[:, :, :], X, ALU.add)
                    dve.tensor_reduce(slot_f[:, :, 1], place2[:, :, :], X, ALU.add).then_inc(slot_f_done, 1)
                    dve.tensor_copy(z[:, :, D:D + 1].bitcast(U32), token[:, :].unsqueeze(2))
                    dve.wait_ge(slot_f_done, q + 1)
                    dve.tensor_copy(slot[:, :, :], slot_f[:, :, :]).then_inc(slot_done, 1)

            def tail(q, j):
                if j == 4:
                    router(q, 0)
                if j == 5:
                    router(q, 1)
                if j == 6:
                    router(q, 2)

            def batch(b, has_tail):
                last = isinstance(b, int) and b == B - 1
                for j in range(T):
                    n = T * b + j
                    dve.wait_ge(s_done, n + 1)
                    dve.tensor_reduce(neg_max[:, j:j + 1], s_ps[j % 2][:, :], X, ALU.max, negate=True).then_inc(max_done, 1)
                    if j:
                        row_sum(b, j - 1)
                    if j >= 2:
                        p_low(b, j - 2)
                    if has_tail:
                        tail(b - 1, j)
                row_sum(b, T - 1)
                p_low(b, T - 2)
                p_low(b, T - 1)
                if not last:
                    ln1(b + 1)
                for t in range(T):
                    m = T * b + t
                    c_step(m, t)
                    if t:
                        z_step(m - 1, t - 1)
                    offset(mv_c, rstd_c, off_c, c_rstd, c_off, t, m)
                    if t:
                        offset(mv_z, rstd_z, off_z, z_rstd, z_off, t - 1, m - 1)
                        if not last:
                            yT_low(b + 1, t - 1)
                if not last:
                    yT_low(b + 1, T - 1)
                z_step(m, T - 1)
                offset(mv_z, rstd_z, off_z, z_rstd, z_off, T - 1, m)

            ln1(0)
            for t in range(T):
                yT_low(0, t)
            dve.wait_ge(consts, NCONST)
            batches(dve, batch)
            for j in range(T):
                tail(B - 1, j)

            lists_at = tab["cnt"]
            dve.wait_ge(slot_done, B)
            dve.tensor_tensor(pad_f[:, :, :], carry[:, :].unsqueeze(2).broadcast_to([P, E, 2]),
                              lane[:, :].unsqueeze(1).broadcast_to([P, E, 2]), ALU.add).then_inc(tab_step, 1)
            dve.scalar_tensor_tensor(lists_at[:, :], rev[0:1, :], float(CAP), carry[0:1, :],
                                     ALU.mult, ALU.add).then_inc(tab_step, 1)
            dve.wait_ge(tab_step, 3)
            dve.tensor_copy(pad_at[:, :, :], pad_f[:, :, :]).then_inc(pads_at, 1)
            dve.tensor_scalar(tab_i[:, :], lists_at[:, :], float(SLOT - 1 - E * CAP), None, ALU.add).then_inc(tab_step, 1)
            dve.wait_ge(tab_step, 4)
            dve.tensor_scalar(tab_i2[:, :], tab_i[:, :], SLOT.bit_length() - 1, None, ALU.logical_shift_right).then_inc(tab_step, 1)
            dve.wait_ge(tab_step, 5)
            dve.tensor_copy(tab["tiles"][:, :], tab_i2[:, :]).then_inc(tab_step, 1)
            dve.wait_ge(tab_step, 6)
            dve.tensor_tensor_scan(tab["end"][:, :], tab["ones"][:, :], tab["tiles"][:, :], 0.0, ALU.mult, ALU.add).then_inc(tab_step, 1)
            dve.wait_ge(tab_step, 7)
            dve.tensor_tensor(tab_big[:, :, :], tab["g"][:, :].unsqueeze(2).broadcast_to([1, G, E]),
                              tab["end"][:, :].unsqueeze(1).broadcast_to([1, G, E]), ALU.is_ge).then_inc(tab_step, 1)
            dve.wait_ge(tab_step, 8)
            dve.tensor_reduce(tab_e[:, :], tab_big[:, :, :], X, ALU.add)
            dve.tensor_tensor(tab_big2[:, :, :], tab_big[:, :, :],
                              tab["tiles"][:, :].unsqueeze(1).broadcast_to([1, G, E]), ALU.mult).then_inc(tab_step, 1)
            dve.wait_ge(tab_step, 9)
            dve.tensor_reduce(tab_k[:, :], tab_big2[:, :, :], X, ALU.add).then_inc(tab_step, 1)
            dve.wait_ge(tab_step, 10)
            dve.tensor_tensor(tab_r[:, :], tab["g"][:, :], tab_k[:, :], ALU.subtract).then_inc(tab_step, 1)
            dve.tensor_scalar(tab_c[:, :], tab_e[:, :], float(CAP), None, ALU.mult).then_inc(tab_step, 1)
            dve.wait_ge(tab_step, 12)
            dve.scalar_tensor_tensor(tile_row[:, :], tab_r[:, :], float(SLOT), tab_c[:, :], ALU.mult, ALU.add)
            dve.tensor_scalar(tile_e[:, :], tab_e[:, :], float(E - 1), None, ALU.min).then_inc(tab_done, 1)

            for i in range(STAGES):
                e, lo, hi = i // 2, (w2_lo if i % 2 else w1_lo), (w2_hi if i % 2 else w1_hi)
                dve.wait_ge(whi_done, i + 1)
                dve.scalar_tensor_tensor(lo[:, e, :], stage[:, i % 4, :], WSCALE, hi[:, e, :],
                                         ALU.mult, ALU.subtract).then_inc(wlo_done, 1)
            dve.wait_ge(b_in, 32)
            dve.wait_ge(tab_done, 1)

            def slots_low(g, par):
                for c in range(2):
                    dve.wait_ge(shi_done, 2 * g + c + 1)
                    cols = slice(c * HALF, (c + 1) * HALF)
                    dve.tensor_tensor(s_lo[:, par, cols], tr_ps[c][:, :], s_hi[:, par, cols], ALU.subtract).then_inc(slo_done, 1)
                dve.tensor_copy(who_all[:, bass.ds(SH * g, SH)].unsqueeze(2), zin[:, par, :, D:D + 1].bitcast(U32)).then_inc(who_in, 1)

            def split_hidden(g, par):
                dve.wait_ge(gelu_done, MH * (g + 1))
                if not isinstance(g, int) or g >= 2:
                    dve.wait_ge(ye_done, SH * (g - 1))
                dve.tensor_copy(h_hi[:, par, :], h32[:, par, :]).then_inc(hhi_done, 1)
                dve.wait_ge(hhi_done, g + 1)
                dve.tensor_tensor(h_lo[:, par, :], h32[:, par, :], h_hi[:, par, :], ALU.subtract).then_inc(hlo_done, 1)

            def expert_out(g, par):
                at = dve.value_load(tile_e[0:1, bass.ds(g, 1)], min_val=0, max_val=E - 1) * D
                if not isinstance(g, int) or g >= 2:
                    dve.wait_ge(added, 16 * SH * (g - 1))
                dve.wait_ge(who_in, g + 1)
                dve.tensor_copy(who[:, par, :], who_all[:, bass.ds(SH * g, SH)]).then_inc(who_done, 1)
                for s in range(SH):
                    dve.wait_ge(ye_done, SH * g + s + 1)
                    dve.scalar_tensor_tensor(yo[:, par, s, :], y_ps[par][s][:, :], 1.0 / WSCALE,
                                             b2_all[:, bass.ds(at, D)], ALU.mult, ALU.add).then_inc(yo_done, 1)

            def step(s, par=None):
                par = s % 2 if par is None else par
                if not isinstance(s, int) or s + 1 < G:
                    slots_low(s + 1, 1 - par)
                if not isinstance(s, int) or s < G:
                    split_hidden(s, par)
                if not isinstance(s, int) or s >= 1:
                    expert_out(s - 1, 1 - par)
            slots_low(0, 0)
            expert_steps(dve, step)

            def final(q, par):
                w = tok_w[:, bass.ds(QT * q, QT)]
                half = (8 * (q - par)) if not isinstance(q, int) else 16 * (q // 2)
                dve.wait_ge(fin_in[par], 2 * half + 32)
                for t in range(QT):
                    last = dve.bn_stats(st_f[:, par, t, :], fin_a[:, par, t, :])
                last.then_inc(f_stats, 1)
                dve.tensor_tensor(w_sq[:, par, :], w, w, ALU.mult).then_inc(f_sq, 1)
                dve.wait_ge(f_stats, q + 1)
                dve.nop(nofuse=True)
                for t in range(QT):
                    last = dve.bn_aggr(mv_f[:, par, t, :], st_f[:, par, t, :])
                last.then_inc(f_mv, 1)
                dve.wait_ge(f_mv, q + 1)
                dve.wait_ge(f_sq, q + 1)
                dve.tensor_tensor(var_f[:, par, :], mv_f[:, par, :, 1], w_sq[:, par, :], ALU.mult).then_inc(f_var, 1)
                dve.wait_ge(f_var, q + 1)
                dve.tensor_scalar(ve_f[:, par, :], var_f[:, par, :], EPS, None, ALU.add).then_inc(f_ve, 1)
                dve.wait_ge(f_rstd, q + 1)
                dve.tensor_tensor(mul_f[:, par, :], rstd_f[:, par, :], w, ALU.mult).then_inc(f_mul, 1)
                dve.wait_ge(f_mul, q + 1)
                dve.scalar_tensor_tensor(off_f[:, par, :], mv_f[:, par, :, 0], -1.0, mul_f[:, par, :],
                                         ALU.mult, ALU.mult).then_inc(f_off, 1)
            with dve.Fori(0, NF // 2) as i:
                final(2 * i, 0)
                final(2 * i + 1, 1)

        @block.tensor
        def _(pe):
            def transpose_y(q, t):
                n = T * q + t
                pe.wait_ge(y_done, n + 1)
                if not isinstance(n, int) or n:
                    pe.wait_ge(yT_lo_done, n)
                for k in range(KD):
                    last = pe.transpose(t_ps[:, k * P:(k + 1) * P], y[:, t, k * P:(k + 1) * P], ident[:, :])
                last.then_inc(yT_done, 1)

            def scores(b, j):
                n = T * b + j
                if j == 0:
                    pe.wait_ge(yT_lo_done, T * (b + 1))
                if not isinstance(n, int) or n >= 2:
                    pe.wait_ge(exp_done, n - 1)
                row = s_ps[j % 2]
                mine = slice(j * P, (j + 1) * P)
                chunks = [(max(j * P, c * HALF), (c + 1) * HALF) for c in range(2) if (c + 1) * HALF > j * P]
                for lo, hi in chunks:
                    for k in range(KD):
                        for i, (l, r) in enumerate(((yT_hi, yT_hi), (yT_hi, yT_lo), (yT_lo, yT_hi))):
                            last = pe.matmul(row[:, lo:hi], l[:, k, mine], r[:, k, lo:hi],
                                             start=(k == 0 and i == 0), stop=(k == KD - 1 and i == 2))
                if j:
                    pe.wait_ge(above_done, (T - 1) * b + j)
                for i in range(j):
                    last = pe.transpose(row[:, i * P:(i + 1) * P],
                                        above[i][:, (j - i - 1) * P:(j - i) * P], ident[:, :])
                last.then_inc(s_done, 1)

            def context(b, t, js):
                m = T * b + t
                if 0 in js and (not isinstance(m, int) or m >= 2):
                    pe.wait_ge(ctxn_done, m - 1)
                rows = slice(t * P, (t + 1) * P)
                for j in js:
                    if t < 2:
                        pe.wait_ge(plo_done, T * b + j + 1)
                        pe.wait_ge(ylo_done, T * b + j + 1)
                    for i, (l, r) in enumerate(((p_hi, y_hi), (p_hi, y_lo), (p_lo, y_hi))):
                        last = pe.matmul(c_ps[t % 2][:, :], l[:, j, rows], r[:, j, :],
                                         start=(j == 0 and i == 0), stop=(j == T - 1 and i == 2))
                if T - 1 in js:
                    last.then_inc(pv_done, 1)

            def transpose_z(q, t, routed):
                m = T * q + t
                pe.wait_ge(z_done, m + 1)
                if not isinstance(m, int) or m:
                    pe.wait_ge(lgT_done, m)
                if t == 0 and routed:
                    pe.wait_ge(slot_done, q)
                for k in range(KD):
                    last = pe.transpose(z_ps[:, k * P:(k + 1) * P], z[:, t, k * P:(k + 1) * P], ident[:, :])
                last.then_inc(ztr_done, 1)

            def logits(q, t):
                pe.wait_ge(zT_done, T * q + t + 1)
                for k in range(KD):
                    last = pe.matmul(z_ps[0:E, 0:P], gate[:, k, :], zT[:, k * P:(k + 1) * P],
                                     start=(k == 0), stop=(k == KD - 1))
                last.then_inc(gate_done, 1)

            def tail(q, j):
                if j == 0:
                    logits(q, T - 3)
                    transpose_z(q, T - 2, False)
                if j == 1:
                    logits(q, T - 2)
                    transpose_z(q, T - 1, False)
                if j == 2:
                    logits(q, T - 1)
                if j == 3:
                    pe.wait_ge(lgT_done, T * (q + 1))
                    pe.nop(nofuse=True)
                    for t in range(T):
                        last = pe.transpose(z_ps[:, t * E:(t + 1) * E], lgT[:, t * P:(t + 1) * P], ident[0:E, 0:E])
                    last.then_inc(lg_ready, 1)
                if j == 5:
                    pe.wait_ge(chosen_done, q + 1)
                    flat = chosen[:, :, :].rearrange("p t e -> p (t e)")
                    W = T * E
                    pe.matmul(z_ps[:, W:2 * W], before[:, :], flat, start=True, stop=False, skip_group_check=True)
                    for s in range(1, T):
                        pe.matmul(z_ps[:, W + s * E:2 * W], ones[:, :], flat[:, 0:W - s * E], start=False,
                                  stop=(s == T - 1), skip_group_check=True)
                    for s in range(T):
                        last = pe.matmul(z_ps[:, 2 * W:2 * W + E], ones[:, :], flat[:, s * E:(s + 1) * E],
                                         start=(s == 0), stop=(s == T - 1), skip_group_check=True)
                    last.then_inc(rank_done, 1)

            def batch(b, has_tail):
                last = isinstance(b, int) and b == B - 1
                for j in range(T):
                    scores(b, j)
                    if has_tail:
                        tail(b - 1, j)
                early = range(T - 1)
                context(b, 0, early)
                context(b, 1, early)
                context(b, 0, [T - 1])
                context(b, 1, [T - 1])
                if not last:
                    transpose_y(b + 1, 0)
                for t in range(2, T):
                    context(b, t, range(T))
                    if t >= 3:
                        logits(b, t - 3)
                    if not last:
                        transpose_y(b + 1, t - 1)
                    transpose_z(b, t - 2, has_tail)
                if not last:
                    transpose_y(b + 1, T - 1)

            pe.wait_ge(consts, NCONST)
            pe.wait_ge(dve_consts, 2)
            pe.wait_ge(const_dma, 16)
            for t in range(T):
                transpose_y(0, t)
            batches(pe, batch)
            for j in range(T):
                tail(B - 1, j)

            pe.wait_ge(wlo_done, STAGES)
            pe.wait_ge(tab_done, 1)
            pe.wait_ge(rank_done, B)
            pe.wait_ge(slot_done, B)

            def transpose_slots(g, par):
                odd = g % 2 if isinstance(g, int) else par
                count = (g // 2 + 1) * 16 if isinstance(g, int) else 8 * (g - par) + 16
                pe.wait_ge(zin_in[odd], count)
                for c in range(2):
                    if not isinstance(g, int) or g:
                        pe.wait_ge(slo_done, 2 * g - 1 + c)
                    for kk in range(2):
                        k = 2 * c + kk
                        for s in range(SH):
                            at = kk * SLOT + s * P
                            last = pe.transpose(tr_ps[c][:, at:at + P], zin[:, par, s, k * P:(k + 1) * P], ident[:, :])
                    last.then_inc(tr_done, 1)

            def up(g, par):
                e = pe.value_load(tile_e[0:1, bass.ds(g, 1)], min_val=0, max_val=E - 1)
                pe.wait_ge(slo_done, 2 * g + 2)
                if not isinstance(g, int) or g >= 2:
                    pe.wait_ge(gelu_done, MH * (g - 1))
                for m in range(MH):
                    for k in range(KD):
                        cols = slice(k * H + m * P, k * H + (m + 1) * P)
                        hi = w1_hi[:, bass.ds(e, 1), cols].rearrange("p e c -> p (e c)")
                        lo = w1_lo[:, bass.ds(e, 1), cols].rearrange("p e c -> p (e c)")
                        rows = slice(k * SLOT, (k + 1) * SLOT)
                        for i, (l, r) in enumerate(((hi, s_hi), (hi, s_lo), (lo, s_hi))):
                            last = pe.matmul(h_ps[par][:, m * SLOT:(m + 1) * SLOT], l, r[:, par, rows],
                                             start=(k == 0 and i == 0), stop=(k == KD - 1 and i == 2))
                last.then_inc(h_done, 1)

            def down(g, par):
                e = pe.value_load(tile_e[0:1, bass.ds(g, 1)], min_val=0, max_val=E - 1)
                pe.wait_ge(hlo_done, g + 1)
                for s in range(SH):
                    if not isinstance(g, int) or g >= 2:
                        pe.wait_ge(yo_done, SH * (g - 2) + s + 1)
                    for m in range(MH):
                        hi = w2_hi[:, bass.ds(e, 1), m * D:(m + 1) * D].rearrange("p e c -> p (e c)")
                        lo = w2_lo[:, bass.ds(e, 1), m * D:(m + 1) * D].rearrange("p e c -> p (e c)")
                        cols = slice(m * SLOT + s * P, m * SLOT + (s + 1) * P)
                        for i, (l, r) in enumerate(((h_hi, hi), (h_hi, lo), (h_lo, hi))):
                            last = pe.matmul(y_ps[par][s][:, :], l[:, par, cols], r,
                                             start=(m == 0 and i == 0), stop=(m == MH - 1 and i == 2))
                    last.then_inc(ye_done, 1)

            def step(s, par=None):
                par = s % 2 if par is None else par
                if not isinstance(s, int) or s + 1 < G:
                    transpose_slots(s + 1, 1 - par)
                if not isinstance(s, int) or s < G:
                    up(s, par)
                if not isinstance(s, int) or s >= 1:
                    down(s - 1, 1 - par)
            transpose_slots(0, 0)
            expert_steps(pe, step)


_INS = ["L0_attn_x", "L0_ffn_gate_w", "L0_ffn_w1", "L0_ffn_b1", "L0_ffn_w2", "L0_ffn_b2"]


def kernel(**inputs):
    import numpy as _np
    import concourse.bacc as _bacc
    from concourse.bass_utils import run_bass_kernel_spmd as _run

    nc = _bacc.Bacc("TRN2", target_bir_lowering=False, num_devices=1)
    arrays, args = {}, []
    for name in _INS:
        a = _np.ascontiguousarray(inputs[name])
        arrays[f"in_{name}"] = a
        args.append(nc.dram_tensor(f"in_{name}", a.shape, mybir.dt.from_np(a.dtype), kind="ExternalInput").ap())
    result = nc.dram_tensor("out_0", inputs["L0_attn_x"].shape, F32, kind="ExternalOutput").ap()
    attention_then_experts(nc, *args, result)
    r = _run(nc, [arrays], core_ids=[0])
    return r.results[0]["out_0"]
```

```python
from contextlib import ExitStack

import numpy as np

import concourse.bass as bass
from concourse import mybir

F32 = mybir.dt.float32
F16 = mybir.dt.float16
U32 = mybir.dt.uint32
I32 = mybir.dt.int32
ALU = mybir.AluOpType
ACT = mybir.ActivationFunctionType
X = mybir.AxisListType.X

P = 128
SLOT = 256
EPS = 1e-5
PSCALE = 1024.0
WSCALE = 64.0
FAR = -1e30


def attention_then_experts(nc, x, gate_w, w1, b1, w2, b2, out):
    B, S, D = x.shape
    E, _, H = w1.shape
    T = S // P
    KD = D // P
    MH = H // P
    NTOK = B * S
    NT = B * T
    CAP = NTOK + SLOT
    G = 2 * NTOK // SLOT + E - 1
    ROW = D + 8
    HALF = 512
    assert T == 8 and KD == 4 and S == 2 * HALF and D == HALF and MH == 2 and G % 2 == 1 and B % 2 == 0 and B >= 6

    x_v = x.rearrange("b (t p) d -> b p t d", p=P)
    xt_v = x.rearrange("b (t p) d -> (b t) p d", p=P)
    out_v = out.rearrange("b (t p) d -> p (b t) d", p=P)
    lists = nc.dram_tensor("slot_lists", (E * CAP + (E - 1) * SLOT, ROW), F32, kind="Internal").ap()
    acc = nc.dram_tensor("expert_sum", (NTOK + SLOT, D), F32, kind="Internal").ap()
    mid = nc.dram_tensor("after_attention", (NTOK, D), F32, kind="Internal").ap()
    mid_t = mid.rearrange("(n p) d -> n p d", p=P)
    mid_v = mid.rearrange("(n p) d -> p n d", p=P)
    acc_t = acc.rearrange("(n p) d -> n p d", p=P)
    acc_v = acc.rearrange("(n p) d -> p n d", p=P)

    with ExitStack() as ctx:
        def sem(name):
            return ctx.enter_context(nc.semaphore(name))

        def sb(name, shape, dt, where=ctx):
            return where.enter_context(nc.sbuf_tensor(name, shape, dt))

        def bank(name, where=ctx, shape=(P, HALF)):
            return where.enter_context(nc.psum_tensor(name, list(shape), F32))

        ident = sb("ident", [P, P], F32)
        before = sb("before", [P, P], F16)
        ones = sb("ones", [P, P], F16)
        pow_exp = sb("pow_exp", [P, T], F32)
        rev = sb("rev", [P, E], F32)
        gate = sb("gate", [P, KD, E], F32)
        b1_col = sb("b1_col", [P, E * MH], F32)
        tok_w = sb("tok_w", [P, NT], F32)
        pad = sb("pad", [P, 2, ROW], F32)
        token = sb("token", [P, T], F32)
        carry = sb("carry", [P, E], F32)
        lg = sb("lg", [P, T, E], F32)
        lg2 = sb("lg2", [P, T, E], F32)
        lgd = sb("lgd", [P, T, E], F32)
        lge = sb("lge", [P, T, E], F32)
        eq = sb("eq", [P, T, E], F32)
        first = sb("first", [P, T, E], F32)
        second = sb("second", [P, T, E], F32)
        chosen = sb("chosen", [P, T, E], F16)
        gnum = sb("gnum", [P, T, E], F32)
        place = sb("place", [P, T, E], F32)
        place1 = sb("place1", [P, T, E], F32)
        place2 = sb("place2", [P, T, E], F32)
        top = sb("top", [P, 6, T], F32)
        slot_f = sb("slot_f", [P, T, 2], F32)
        slot = sb("slot", [P, 2, T, 2], U32)
        pad_f = sb("pad_f", [P, E, 2], F32)
        pad_at = sb("pad_at", [P, E, 2], U32)
        lane = sb("lane", [P, 2], F32)
        st_x = sb("st_x", [P, T, 6], F32)
        mv_x = sb("mv_x", [P, T, 2], F32)
        var_x = sb("var_x", [P, T], F32)
        rstd_x = sb("rstd_x", [P, T], F32)
        off_x = sb("off_x", [P, T], F32)
        st_c = sb("st_c", [P, T, 6], F32)
        mv_c = sb("mv_c", [P, T, 2], F32)
        var_c = sb("var_c", [P, T], F32)
        rstd_c = sb("rstd_c", [P, T], F32)
        off_c = sb("off_c", [P, T], F32)
        st_z = sb("st_z", [P, T, 6], F32)
        mv_z = sb("mv_z", [P, T, 2], F32)
        var_z = sb("var_z", [P, T], F32)
        rstd_z = sb("rstd_z", [P, T], F32)
        off_z = sb("off_z", [P, T], F32)
        neg_max = sb("neg_max", [P, T], F32)
        psum_row = sb("psum_row", [P, T], F32)
        psum_sc = sb("psum_sc", [P, T], F32)
        pinv = sb("pinv", [P, T], F32)
        tab = {n: sb(f"tab_{n}", [1, w], F32) for n, w in
               (("cnt", E), ("tiles", E), ("ones", E), ("end", E), ("g", G))}
        tab_big = sb("tab_big", [1, G, E], F32)
        tab_big2 = sb("tab_big2", [1, G, E], F32)
        tab_e = sb("tab_e", [1, G], F32)
        tab_k = sb("tab_k", [1, G], F32)
        tab_c = sb("tab_c", [1, G], F32)
        tab_r = sb("tab_r", [1, G], F32)
        tab_i = sb("tab_i", [1, E], I32)
        tab_i2 = sb("tab_i2", [1, E], I32)
        tile_row = sb("tile_row", [1, G], I32)
        tile_e = sb("tile_e", [1, G], I32)

        with ExitStack() as a:
            y = sb("y", [P, 2, T, D], F32, a)
            y_hi = sb("y_hi", [P, 2, T, D], F16, a)
            y_lo = sb("y_lo", [P, T, D], F16, a)
            yT_hi = sb("yT_hi", [P, KD, S], F16, a)
            yT_lo = sb("yT_lo", [P, KD, S], F16, a)
            p_hi = sb("p_hi", [P, T, S], F16, a)
            p_lo = sb("p_lo", [P, T, S], F16, a)
            p32 = sb("p32", [P, 3, S], F32, a)
            above = [sb(f"above{j}", [P, S - P * (j + 1)], F32, a) for j in range(T - 1)]
            z = sb("z", [P, 2, T, ROW], F32, a)
            ctxn = sb("ctxn", [P, 2, D], F32, a)
            xres = sb("xres", [P, 2, D], F32, a)
            x1 = sb("x1", [P, 2, D], F32, a)
            zT = sb("zT", [P, D], F32, a)
            lgT = sb("lgT", [E, S], F32, a)
        with ExitStack() as a:
            w1_hi = sb("w1_hi", [P, E, KD * H], F16, a)
            w1_lo = sb("w1_lo", [P, E, KD * H], F16, a)
            w2_hi = sb("w2_hi", [P, E, MH * D], F16, a)
            w2_lo = sb("w2_lo", [P, E, MH * D], F16, a)
            b2_all = sb("b2_all", [P, E * D], F32, a)
            zin = sb("zin", [P, 2, 2, ROW], F32, a)
            s_hi = sb("s_hi", [P, 2, KD * SLOT], F16, a)
            s_lo = sb("s_lo", [P, 2, KD * SLOT], F16, a)
            h32 = sb("h32", [P, 2, MH * SLOT], F32, a)
            h_hi = sb("h_hi", [P, 2, MH * SLOT], F16, a)
            h_lo = sb("h_lo", [P, 2, MH * SLOT], F16, a)
            yo = sb("yo", [P, 2, 2, D], F32, a)
            who_all = sb("who_all", [P, 2 * G], U32, a)
            who = sb("who", [P, 2, 2], U32, a)
            with ExitStack() as b:
                stage = sb("stage", [P, 4, KD * H], F32, b)
            QT = 4
            FB = 4
            fin_x = sb("fin_x", [P, FB, QT, D], F32, a)
        with ExitStack() as a:
            fin_a = sb("fin_a", [P, FB, QT, D], F32, a)
            st_f = sb("st_f", [P, FB, QT, 6], F32, a)
            mv_f = sb("mv_f", [P, FB, QT, 2], F32, a)
            w_sq = sb("w_sq", [P, FB, QT], F32, a)
            var_f = sb("var_f", [P, FB, QT], F32, a)
            ve_f = sb("ve_f", [P, FB, QT], F32, a)
            rstd_f = sb("rstd_f", [P, FB, QT], F32, a)
            mul_f = sb("mul_f", [P, FB, QT], F32, a)
            off_f = sb("off_f", [P, FB, QT], F32, a)

        with ExitStack() as a:
            s_ps = [bank(f"s_ps{i}", a, (P, S)) for i in range(2)]
            c_ps = [bank(f"c_ps{i}", a) for i in range(2)]
            t_ps = bank("t_ps", a)
            z_ps = bank("z_ps", a)
            yt_ps = [t_ps[:, :], s_ps[1][:, HALF:S]]
        with ExitStack() as a:
            tr_ps = [bank(f"tr_ps{i}", a) for i in range(2)]
            h_ps = [bank(f"h_ps{i}", a) for i in range(2)]
            y_ps = [[bank(f"y_ps{i}{s}", a) for s in range(2)] for i in range(2)]

        consts = sem("consts")
        dve_consts = sem("dve_consts")
        const_dma = sem("const_dma")
        x_in = [sem(f"x_in{i}") for i in range(2)]
        xres_in = [sem(f"xres_in{i}") for i in range(2)]
        mid_out = [sem(f"mid_out{i}") for i in range(2)]
        zero_out = sem("zero_out")
        ln1_stats, ln1_mv, ln1_var, ln1_rstd, ln1_off = (sem(f"ln1_{n}") for n in ("stats", "mv", "var", "rstd", "off"))
        y_done = sem("y_done")
        yT_done, yT_hi_done, yT_lo_done = sem("yT_done"), sem("yT_hi_done"), sem("yT_lo_done")
        yhi_done, ylo_done = sem("yhi_done"), sem("ylo_done")
        s_done, above_done, exp_done = sem("s_done"), sem("above_done"), sem("exp_done")
        max_done, sum_done, inv_done = sem("max_done"), sem("sum_done"), sem("inv_done")
        phi_done, plo_done, pv_done = sem("phi_done"), sem("plo_done"), sem("pv_done")
        c_stats, c_mv, c_var, c_rstd, c_off = (sem(f"c_{n}") for n in ("stats", "mv", "var", "rstd", "off"))
        z_stats, z_mv, z_var, z_rstd, z_off = (sem(f"z_{n}") for n in ("stats", "mv", "var", "rstd", "off"))
        ctxn_done, x1_done, z_done = sem("ctxn_done"), sem("x1_done"), sem("z_done")
        ztr_done, zT_done, gate_done, lgT_done = sem("ztr_done"), sem("zT_done"), sem("gate_done"), sem("lgT_done")
        lg_ready, lgd_done, lge_done = sem("lg_ready"), sem("lgd_done"), sem("lge_done")
        route, chosen_done, rank_done, slot_done = sem("route"), sem("chosen_done"), sem("rank_done"), sem("slot_done")
        scat = [[sem(f"scat{i}_{t}") for t in range(T)] for i in range(2)]
        slot_f_done = sem("slot_f_done")
        pads_at, pads_out, tab_step, tab_done = sem("pads_at"), sem("pads_out"), sem("tab_step"), sem("tab_done")
        w_in = [sem(f"w_in{i}") for i in range(4)]
        whi_done, wlo_done, b_in = sem("whi_done"), sem("wlo_done"), sem("b_in")
        zin_in = [sem(f"zin_in{i}") for i in range(2)]
        tr_done, shi_done, slo_done = sem("tr_done"), sem("shi_done"), sem("slo_done")
        who_in, who_done = sem("who_in"), sem("who_done")
        h_done, gelu_done, hhi_done, hlo_done = sem("h_done"), sem("gelu_done"), sem("hhi_done"), sem("hlo_done")
        ye_done, yo_done = sem("ye_done"), sem("yo_done")
        added = sem("added")
        fin_a_in = [sem(f"fin_a_in{i}") for i in range(FB)]
        fin_x_in = [sem(f"fin_x_in{i}") for i in range(FB)]
        f_stats, f_mv, f_sq, f_var, f_ve, f_rstd, f_mul, f_off = (
            sem(f"f_{n}") for n in ("stats", "mv", "sq", "var", "ve", "rstd", "mul", "off"))
        f_norm, f_sum = sem("f_norm"), sem("f_sum")
        fin_out = [sem(f"fin_out{i}") for i in range(FB)]

        NCONST = 12
        ROUTE = 20
        TAB = 9
        SH = SLOT // P
        STAGES = 2 * E
        NF = NT // QT

        def batches(eng, one):
            one(0, 0, 0)
            one(1, 0, 1)
            with eng.Fori(1, B // 2 - 1) as h:
                one(2 * h, h, 0)
                one(2 * h + 1, h, 1)
            one(B - 2, B // 2 - 1, 0)
            one(B - 1, B // 2 - 1, 1)

        def is_first(b):
            return isinstance(b, int) and b == 0

        def is_last(b):
            return isinstance(b, int) and b == B - 1

        Y_AHEAD = {2: (0, 1), 3: (2,), 4: (3,), 5: (4,), 6: (5,), 7: (6, 7)}

        def expert_steps(eng, one):
            for s in range(3):
                one(s)
            with eng.Fori(0, (G - 5) // 2) as i:
                one(2 * i + 3, 1)
                one(2 * i + 4, 0)
            for s in range(G - 2, G + 1):
                one(s)

        block = ctx.enter_context(nc.Block())

        @block.sync
        def _(sp):
            sp.dma_start(y[:, 0, :, :], x_v[0]).then_inc(x_in[0], 16)
            sp.dma_start(gate[:, :, :], gate_w.rearrange("(k p) e -> p k e", p=P)).then_inc(const_dma, 16)
            sp.dma_start(b1_col[:, :], b1.rearrange("e (m p) -> p (e m)", p=P),
                         allow_slow_non_contiguous=True).then_inc(b_in, 16)
            for i in range(2):
                sp.dma_start(xres[:, i, :], xt_v[i]).then_inc(xres_in[i], 16)
            sp.dma_start(y[:, 1, :, :], x_v[1]).then_inc(x_in[1], 16)
            sp.wait_ge(consts, NCONST)
            for n in range(NTOK // P + SH):
                sp.dma_start(acc_t[n], pad[:, 0, 0:D]).then_inc(zero_out, 16)
            for n in range(E - 1):
                at = E * CAP + n * SLOT
                sp.dma_start(lists[at:at + SLOT, :].rearrange("(s p) r -> p s r", p=P),
                             pad[:, :, :]).then_inc(zero_out, 16)

            def batch(b, h, par):
                last = is_last(b)
                if not (isinstance(b, int) and b >= B - 2):
                    sp.wait_ge(yT_done, T * (b + 1))
                    sp.wait_ge(ylo_done, T * (b + 1))
                    sp.dma_start(y[:, par, :, :], x_v[bass.ds(b + 2, 1)].rearrange("b p t d -> p (b t) d")
                                 ).then_inc(x_in[par], 16)
                for t in range(T):
                    m = T * b + t
                    sp.wait_ge(x1_done, m + 1)
                    sp.dma_start(mid_t[bass.ds(m, 1)].rearrange("n p d -> p (n d)"),
                                 x1[:, t % 2, :]).then_inc(mid_out[t % 2], 16)
                    if not (last and t >= T - 2):
                        sp.dma_start(xres[:, t % 2, :], xt_v[bass.ds(m + 2, 1)].rearrange("n p d -> p (n d)")
                                     ).then_inc(xres_in[t % 2], 16)
            batches(sp, batch)

            sp.wait_ge(pv_done, NT)
            sp.wait_ge(ctxn_done, NT)
            for t in range(T):
                sp.wait_ge(scat[0][t], 32 * B // 2)
            sp.dma_start(b2_all[:, :], b2.rearrange("e d -> (e d)").partition_broadcast(P)).then_inc(b_in, 16)
            for i in range(STAGES):
                if i >= 4:
                    sp.wait_ge(wlo_done, i - 3)
                e, second_w = i // 2, i % 2
                src = (w2[e].rearrange("(m p) d -> p m d", p=P) if second_w
                       else w1[e].rearrange("(k p) h -> p k h", p=P))
                sp.dma_start(stage[:, i % 4, :].rearrange("p (k h) -> p k h", k=MH if second_w else KD),
                             src).then_inc(w_in[i % 4], 16)

            for par in range(2):
                for t in range(T):
                    sp.wait_ge(scat[par][t], 32 * B // 2)
            sp.wait_ge(pads_out, 16 * 2 * E)
            sp.wait_ge(zero_out, 16 * (NTOK // P + SH + E - 1))
            sp.wait_ge(tab_done, 1)

            def load_slots(g, par):
                if not isinstance(g, int) or g >= 2:
                    sp.wait_ge(tr_done, 2 * (g - 1))
                    sp.wait_ge(who_in, g - 1)
                row = sp.value_load(tile_row[0:1, bass.ds(g, 1)], min_val=0,
                                    max_val=E * CAP + (E - 2) * SLOT)
                sp.dma_start(zin[:, par, :, :], lists[bass.ds(row, SLOT), :].rearrange("(s p) r -> p s r", p=P)
                             ).then_inc(zin_in[par], 16)
            load_slots(0, 0)
            load_slots(1, 1)
            with sp.Fori(0, (G - 3) // 2) as i:
                load_slots(2 * i + 2, 0)
                load_slots(2 * i + 3, 1)
            load_slots(G - 1, 0)

            def load_residual(i, par):
                sp.dma_start(fin_x[:, par, :, :], mid_v[:, bass.ds(QT * (FB * i + par), QT), :]).then_inc(fin_x_in[par], 16)

            def load_sums(i, par):
                sp.dma_start(fin_a[:, par, :, :], acc_v[:, bass.ds(QT * (FB * i + par), QT), :]).then_inc(fin_a_in[par], 16)

            for i in range(2):
                sp.wait_ge(mid_out[i], 16 * NT // 2)
            sp.wait_ge(wlo_done, STAGES)
            for par in range(FB):
                load_residual(0, par)
            sp.wait_ge(added, 16 * SH * G)
            sp.wait_ge(ye_done, SH * G)
            for par in range(FB):
                load_sums(0, par)
            with sp.Fori(1, NF // FB) as i:
                for par in range(FB):
                    sp.wait_ge(fin_out[par], 16 * i)
                    load_sums(i, par)
                    load_residual(i, par)
            for par in range(FB):
                sp.wait_ge(fin_out[par], 16 * NF // FB)

        @block.gpsimd
        def _(pool):
            pool.memset(ident[:, :], 0.0).then_inc(consts, 1)
            pool.memset(before[:, :], 1.0).then_inc(consts, 1)
            pool.memset(pow_exp[:, :], -0.5).then_inc(consts, 1)
            pool.memset(z[:, :, :, :], 0.0).then_inc(consts, 1)
            pool.memset(pad[:, :, :], 0.0).then_inc(consts, 1)
            pool.wait_ge(consts, 5)
            pool.affine_select(out=ident[:, :], in_=ident[:, :], compare_op=ALU.not_equal, fill=1.0,
                               base=0, pattern=[[-1, P]], channel_multiplier=1).then_inc(consts, 1)
            pool.affine_select(out=before[:, :], in_=before[:, :], compare_op=ALU.is_gt, fill=0.0,
                               base=0, pattern=[[1, P]], channel_multiplier=-1).then_inc(consts, 1)
            pool.iota(token[:, :], pattern=[[P, T]], base=-S, channel_multiplier=1,
                      allow_small_or_imprecise_dtypes=True).then_inc(consts, 1)
            pool.iota(lane[:, :], pattern=[[P, 2]], base=0, channel_multiplier=1,
                      allow_small_or_imprecise_dtypes=True).then_inc(consts, 1)
            pool.iota(carry[:, :], pattern=[[CAP, E]], base=0, channel_multiplier=0,
                      allow_small_or_imprecise_dtypes=True).then_inc(consts, 1)
            pool.iota(rev[:, :], pattern=[[-1, E]], base=E, channel_multiplier=0,
                      allow_small_or_imprecise_dtypes=True).then_inc(consts, 1)
            pool.iota(pad[:, :, D:D + 1].bitcast(U32).rearrange("p s r -> p (s r)"), pattern=[[P, 2]], base=NTOK,
                      channel_multiplier=1).then_inc(consts, 1)
            pool.iota(tab["g"][:, :], pattern=[[1, G]], base=0, channel_multiplier=0,
                      allow_small_or_imprecise_dtypes=True).then_inc(tab_step, 1)

            def power(out, in_, wait, n, done):
                pool.wait_ge(wait, n)
                pool.tensor_tensor(out, in_, pow_exp[:, 0:in_.shape[1]], ALU.pow).then_inc(done, 1)

            def scatter(q, par, t):
                pool.wait_ge(slot_done, q + 1)
                pool.nop(nofuse=True)
                for k in range(2):
                    pool.indirect_dma_start(out=lists, in_=z[:, par, t, :], in_offset=None,
                                            out_offset=bass.IndirectOffsetOnAxis(ap=slot[:, par, t, k:k + 1], axis=0)
                                            ).then_inc(scat[par][t], 16)

            SEND = {2: (0,), 3: (1,), 4: (2, 3), 5: (4,), 6: (5, 6), 7: (7,)}

            def batch(b, h, par):
                for j in range(T):
                    if not is_first(b):
                        pool.wait_ge(pv_done, T * b)
                    pool.wait_ge(yhi_done, T * b + j + 1)
                    pool.tensor_tensor(y_lo[:, j, :], y[:, par, j, :], y_hi[:, par, j, :], ALU.subtract).then_inc(ylo_done, 1)
                if not is_last(b):
                    power(rstd_x[:, :], var_x[:, :], ln1_var, b + 2, ln1_rstd)
                for t in range(T):
                    m = T * b + t
                    power(rstd_c[:, t:t + 1], var_c[:, t:t + 1], c_var, m + 1, c_rstd)
                    if t:
                        power(rstd_z[:, t - 1:t], var_z[:, t - 1:t], z_var, m, z_rstd)
                    pool.wait_ge(ctxn_done, m + 1)
                    half_batch = T // 2
                    pool.wait_ge(xres_in[t % 2], 16 * (half_batch * b + t // 2 + 1))
                    if t >= 2 or not is_first(b):
                        pool.wait_ge(mid_out[t % 2], 16 * (half_batch * b + t // 2))
                        pool.wait_ge(z_done, m - 1)
                    pool.tensor_tensor(x1[:, t % 2, :], xres[:, t % 2, :], ctxn[:, t % 2, :], ALU.add).then_inc(x1_done, 1)
                    if t == T - 1:
                        power(rstd_z[:, t:t + 1], var_z[:, t:t + 1], z_var, m + 1, z_rstd)
                    if not is_first(b):
                        for u in SEND.get(t, ()):
                            scatter(b - 1, 1 - par, u)

            power(rstd_x[:, :], var_x[:, :], ln1_var, 1, ln1_rstd)
            batches(pool, batch)
            for t in range(T):
                scatter(B - 1, 1, t)
            pool.wait_ge(pads_at, 1)
            for e in range(E):
                for s in range(SH):
                    pool.indirect_dma_start(out=lists, in_=pad[:, s, :], in_offset=None,
                                            out_offset=bass.IndirectOffsetOnAxis(ap=pad_at[:, e, s:s + 1], axis=0)
                                            ).then_inc(pads_out, 16)

            def add_rows(g, par):
                pool.wait_ge(who_done, g + 1)
                for s in range(SH):
                    pool.wait_ge(yo_done, SH * g + s + 1)
                    if s == 0 and (not isinstance(g, int) or g):
                        pool.wait_ge(added, 16 * SH * g)
                    pool.nop(nofuse=True)
                    pool.indirect_dma_start(out=acc, in_=yo[:, par, s, :], in_offset=None, compute_op=ALU.add,
                                            out_offset=bass.IndirectOffsetOnAxis(ap=who[:, par, s:s + 1], axis=0)
                                            ).then_inc(added, 16)
            pool.wait_ge(zero_out, 16 * (NTOK // P + SH + E - 1))
            add_rows(0, 0)
            with pool.Fori(0, (G - 3) // 2) as i:
                add_rows(2 * i + 1, 1)
                add_rows(2 * i + 2, 0)
            add_rows(G - 2, 1)
            add_rows(G - 1, 0)

            def final_power(q, par):
                pool.wait_ge(f_ve, q + 1)
                pool.tensor_tensor(rstd_f[:, par, :], ve_f[:, par, :], pow_exp[:, 0:QT], ALU.pow).then_inc(f_rstd, 1)

            def final_add(q, i, par):
                pool.wait_ge(fin_x_in[par], 16 * i + 16)
                pool.wait_ge(f_norm, QT * (q + 1))
                pool.tensor_tensor(fin_x[:, par, :, :], fin_x[:, par, :, :], fin_a[:, par, :, :], ALU.add).then_inc(f_sum, 1)

            def final(i, par, end=False):
                q = FB * i + par
                if not end:
                    final_power(q + 1, (par + 1) % FB)
                final_add(q, i, par)
            final_power(0, 0)
            with pool.Fori(0, NF // FB - 1) as i:
                for par in range(FB):
                    final(i, par)
            for par in range(FB):
                final(NF // FB - 1, par, par == FB - 1)

        @block.scalar
        def _(act):
            def norm_x(q, par, t):
                act.wait_ge(ln1_off, q + 1)
                act.activation(y[:, par, t, :], y[:, par, t, :], ACT.Identity, bias=off_x[:, t:t + 1],
                               scale=rstd_x[:, t:t + 1]).then_inc(y_done, 1)

            def y_high(q, par, t):
                act.wait_ge(y_done, T * q + t + 1)
                act.activation(y_hi[:, par, t, :], y[:, par, t, :], ACT.Copy).then_inc(yhi_done, 1)

            def yT_high(q, t):
                act.wait_ge(yT_done, T * q + t + 1)
                act.activation(yT_hi[:, :, t * P:(t + 1) * P], yt_ps[t % 2].rearrange("p (k c) -> p k c", k=KD),
                               ACT.Copy).then_inc(yT_hi_done, 1)

            def norm_context(b, t):
                act.wait_ge(c_off, T * b + t + 1)
                act.activation(ctxn[:, t % 2, :], c_ps[t % 2][:, :], ACT.Identity, bias=off_c[:, t:t + 1],
                               scale=rstd_c[:, t:t + 1]).then_inc(ctxn_done, 1)

            def norm_z(q, h, par, t):
                act.wait_ge(z_off, T * q + t + 1)
                if not isinstance(q, int) or q >= 2:
                    act.wait_ge(scat[par][t], 32 * h)
                act.activation(z[:, par, t, 0:D], x1[:, t % 2, :], ACT.Identity, bias=off_z[:, t:t + 1],
                               scale=rstd_z[:, t:t + 1]).then_inc(z_done, 1)

            def copy_zT(q, t):
                act.wait_ge(ztr_done, T * q + t + 1)
                act.activation(zT[:, :], z_ps[:, :], ACT.Copy).then_inc(zT_done, 1)

            def copy_lgT(q, t):
                act.wait_ge(gate_done, T * q + t + 1)
                act.activation(lgT[:, t * P:(t + 1) * P], z_ps[0:E, 0:P], ACT.Copy).then_inc(lgT_done, 1)

            def p_high(b, j):
                act.wait_ge(inv_done, T * b + j + 1)
                act.activation(p_hi[:, j, :], p32[:, j % 3, :], ACT.Copy, scale=pinv[:, j:j + 1]).then_inc(phi_done, 1)

            def router_exp(q):
                act.wait_ge(lgd_done, q + 1)
                act.activation(lge[:, :, :], lgd[:, :, :], ACT.Exp).then_inc(lge_done, 1)

            def tail(q, h, par, j):
                if j < 3:
                    copy_zT(q, T - 3 + j)
                    copy_lgT(q, T - 3 + j)
                if j == 0:
                    norm_z(q, h, par, T - 1)

            def batch(b, h, par):
                before_h = h if par else h - 1
                for j in range(T):
                    n = T * b + j
                    if not is_first(b):
                        tail(b - 1, before_h, 1 - par, j)
                    act.wait_ge(max_done, n + 1)
                    sp_ = s_ps[j % 2]
                    if j < T - 1:
                        act.activation(above[j][:, :], sp_[:, (j + 1) * P:S], ACT.Copy).then_inc(above_done, 1)
                    if j >= 3:
                        act.wait_ge(plo_done, n - 2)
                    act.activation(p32[:, j % 3, :], sp_[:, :], ACT.Exp, bias=neg_max[:, j:j + 1],
                                   accum_out=psum_row[:, j:j + 1]).then_inc(exp_done, 1)
                    if j:
                        if j == 1 and not is_first(b):
                            act.wait_ge(pv_done, T * b)
                        p_high(b, j - 1)
                p_high(b, T - 1)
                if not is_first(b):
                    router_exp(b - 1)
                AHEAD = 4
                if not is_last(b):
                    for t in range(AHEAD):
                        norm_x(b + 1, 1 - par, t)
                for t in range(1, T + 1):
                    if t >= 4:
                        copy_lgT(b, t - 4)
                    if not is_last(b):
                        for u in Y_AHEAD.get(t, ()):
                            yT_high(b + 1, u)
                    norm_context(b, t - 1)
                    if 3 <= t < T:
                        copy_zT(b, t - 3)
                    if t >= 2:
                        norm_z(b, h, par, t - 2)
                    if not is_last(b):
                        if t - 1 + AHEAD < T:
                            norm_x(b + 1, 1 - par, t - 1 + AHEAD)
                        y_high(b + 1, 1 - par, t - 1)

            for t in range(T):
                norm_x(0, 0, t)
            for t in range(T):
                yT_high(0, t)
                y_high(0, 0, t)
            batches(act, batch)
            for j in range(T):
                tail(B - 1, B // 2 - 1, 1, j)
            router_exp(B - 1)

            for i in range(STAGES):
                e, dst = i // 2, (w2_hi if i % 2 else w1_hi)
                act.wait_ge(w_in[i % 4], 16 * (i // 4 + 1))
                act.activation(dst[:, e, :], stage[:, i % 4, :], ACT.Copy, scale=WSCALE).then_inc(whi_done, 1)
            act.wait_ge(b_in, 32)
            act.wait_ge(tab_done, 1)

            def slots_high(g, par):
                for c in range(2):
                    act.wait_ge(tr_done, 2 * g + c + 1)
                    if c == 0 and (not isinstance(g, int) or g >= 2):
                        act.wait_ge(h_done, g - 1)
                    act.activation(s_hi[:, par, c * HALF:(c + 1) * HALF], tr_ps[c][:, :], ACT.Copy).then_inc(shi_done, 1)

            def gelu(g, par):
                e2 = act.value_load(tile_e[0:1, bass.ds(g, 1)], min_val=0, max_val=E - 1) * MH
                act.wait_ge(h_done, g + 1)
                if not isinstance(g, int) or g >= 2:
                    act.wait_ge(hlo_done, g - 1)
                for m in range(MH):
                    act.activation(h32[:, par, m * SLOT:(m + 1) * SLOT], h_ps[par][:, m * SLOT:(m + 1) * SLOT],
                                   ACT.Gelu, bias=b1_col[:, bass.ds(e2 + m, 1)], scale=1.0 / WSCALE).then_inc(gelu_done, 1)

            def step(s, par=None):
                par = s % 2 if par is None else par
                if not isinstance(s, int) or s + 1 < G:
                    slots_high(s + 1, 1 - par)
                if not isinstance(s, int) or s < G:
                    gelu(s, par)
            slots_high(0, 0)
            expert_steps(act, step)

            def final_norm(q, par):
                act.wait_ge(f_off, q + 1)
                for t in range(QT):
                    act.activation(fin_a[:, par, t, :], fin_a[:, par, t, :], ACT.Identity, bias=off_f[:, par, t:t + 1],
                                   scale=mul_f[:, par, t:t + 1]).then_inc(f_norm, 1)

            def store_final(q, par):
                act.wait_ge(f_sum, q + 1)
                act.dma_start(out_v[:, bass.ds(QT * q, QT), :], fin_x[:, par, :, :]).then_inc(fin_out[par], 16)

            def final(i, par, end=False):
                q = FB * i + par
                if not end:
                    final_norm(q + 1, (par + 1) % FB)
                store_final(q, par)
            final_norm(0, 0)
            with act.Fori(0, NF // FB - 1) as i:
                for par in range(FB):
                    final(i, par)
            for par in range(FB):
                final(NF // FB - 1, par, par == FB - 1)

        @block.vector
        def _(dve):
            dve.memset(ones[:, :], 1.0).then_inc(dve_consts, 1)
            dve.memset(tab["ones"][:, :], 1.0).then_inc(dve_consts, 1)

            def stats(src, st, mv, var, off, rstd, eps, done, i, n):
                stat_s, mv_s, var_s = done
                dve.bn_stats(st[:, i, :], src).then_inc(stat_s, 1)
                dve.wait_ge(stat_s, n + 1)
                dve.nop(nofuse=True)
                dve.bn_aggr(mv[:, i, :], st[:, i, :]).then_inc(mv_s, 1)
                dve.wait_ge(mv_s, n + 1)
                dve.tensor_scalar(var[:, i:i + 1], mv[:, i, 1:2], eps, None, ALU.add).then_inc(var_s, 1)

            def offset(mv, rstd, off, rstd_s, off_s, i, n):
                dve.wait_ge(rstd_s, n + 1)
                dve.scalar_tensor_tensor(off[:, i:i + 1], mv[:, i, 0:1], -1.0, rstd[:, i:i + 1],
                                         ALU.mult, ALU.mult).then_inc(off_s, 1)

            def ln1_stat(q, h, par, tiles):
                dve.wait_ge(x_in[par], 16 * (h + 1))
                for t in tiles:
                    last = dve.bn_stats(st_x[:, t, :], y[:, par, t, :])
                if T - 1 in tiles:
                    last.then_inc(ln1_stats, 1)

            def ln1_moments(q):
                dve.wait_ge(ln1_stats, q + 1)
                dve.nop(nofuse=True)
                for t in range(T):
                    last = dve.bn_aggr(mv_x[:, t, :], st_x[:, t, :])
                last.then_inc(ln1_mv, 1)
                dve.wait_ge(ln1_mv, q + 1)
                dve.tensor_scalar(var_x[:, :], mv_x[:, :, 1], EPS, None, ALU.add).then_inc(ln1_var, 1)

            def ln1_offset(q):
                dve.wait_ge(ln1_rstd, q + 1)
                dve.scalar_tensor_tensor(off_x[:, :], mv_x[:, :, 0], -1.0, rstd_x[:, :], ALU.mult, ALU.mult).then_inc(ln1_off, 1)

            def yT_low(q, t):
                dve.wait_ge(yT_hi_done, T * q + t + 1)
                cols = slice(t * P, (t + 1) * P)
                dve.tensor_tensor(yT_lo[:, :, cols], yt_ps[t % 2].rearrange("p (k c) -> p k c", k=KD),
                                  yT_hi[:, :, cols], ALU.subtract).then_inc(yT_lo_done, 1)

            def c_step(m, t):
                dve.wait_ge(pv_done, m + 1)
                stats(c_ps[t % 2][:, :], st_c, mv_c, var_c, off_c, rstd_c, EPS * PSCALE * PSCALE,
                      (c_stats, c_mv, c_var), t, m)

            def z_step(m, t):
                dve.wait_ge(x1_done, m + 1)
                stats(x1[:, t % 2, :], st_z, mv_z, var_z, off_z, rstd_z, EPS, (z_stats, z_mv, z_var), t, m)

            def row_sum(b, j):
                n = T * b + j
                dve.wait_ge(exp_done, n + 1)
                dve.tensor_scalar(psum_sc[:, j:j + 1], psum_row[:, j:j + 1], 1.0 / PSCALE, None, ALU.mult).then_inc(sum_done, 1)
                dve.wait_ge(sum_done, n + 1)
                dve.reciprocal(pinv[:, j:j + 1], psum_sc[:, j:j + 1]).then_inc(inv_done, 1)

            def p_low(b, j):
                dve.wait_ge(phi_done, T * b + j + 1)
                dve.scalar_tensor_tensor(p_lo[:, j, :], p32[:, j % 3, :], pinv[:, j:j + 1], p_hi[:, j, :],
                                         ALU.mult, ALU.subtract).then_inc(plo_done, 1)

            def wide(col):
                return col.unsqueeze(2).broadcast_to([P, T, E])

            def across(row):
                return row.unsqueeze(1).broadcast_to([P, T, E])

            def router(q, par, part):
                base = ROUTE * q
                flat = "p t e -> p (t e)"
                if part == 0:
                    dve.wait_ge(lg_ready, q + 1)
                    dve.tensor_copy(lg[:, :, :].rearrange(flat), z_ps[:, 0:T * E]).then_inc(route, 1)
                    dve.wait_ge(route, base + 1)
                    dve.tensor_reduce(top[:, 0, :], lg[:, :, :], X, ALU.max).then_inc(route, 1)
                    dve.wait_ge(route, base + 2)
                    dve.tensor_tensor(lgd[:, :, :], lg[:, :, :], wide(top[:, 0, :]), ALU.subtract).then_inc(lgd_done, 1)
                    dve.tensor_tensor(eq[:, :, :], lg[:, :, :], wide(top[:, 0, :]), ALU.is_equal).then_inc(route, 1)
                    dve.wait_ge(route, base + 3)
                    dve.tensor_tensor(gnum[:, :, :], eq[:, :, :], across(rev[:, :]), ALU.mult).then_inc(route, 1)
                    dve.wait_ge(route, base + 4)
                    dve.tensor_reduce(top[:, 1, :], gnum[:, :, :], X, ALU.max).then_inc(route, 1)
                    dve.wait_ge(route, base + 5)
                    dve.tensor_tensor(first[:, :, :], across(rev[:, :]), wide(top[:, 1, :]), ALU.is_equal).then_inc(route, 1)
                    dve.wait_ge(route, base + 6)
                    dve.scalar_tensor_tensor(lg2[:, :, :].rearrange(flat), first[:, :, :].rearrange(flat), FAR,
                                             lg[:, :, :].rearrange(flat), ALU.mult, ALU.add).then_inc(route, 1)
                    dve.wait_ge(route, base + 7)
                    dve.tensor_reduce(top[:, 2, :], lg2[:, :, :], X, ALU.max).then_inc(route, 1)
                    dve.wait_ge(route, base + 8)
                    dve.tensor_tensor(eq[:, :, :], lg2[:, :, :], wide(top[:, 2, :]), ALU.is_equal).then_inc(route, 1)
                    dve.wait_ge(route, base + 9)
                    dve.tensor_tensor(gnum[:, :, :], eq[:, :, :], across(rev[:, :]), ALU.mult).then_inc(route, 1)
                    dve.wait_ge(route, base + 10)
                    dve.tensor_reduce(top[:, 3, :], gnum[:, :, :], X, ALU.max).then_inc(route, 1)
                    dve.wait_ge(route, base + 11)
                    dve.tensor_tensor(second[:, :, :], across(rev[:, :]), wide(top[:, 3, :]), ALU.is_equal).then_inc(route, 1)
                    dve.wait_ge(route, base + 12)
                    dve.tensor_tensor(chosen[:, :, :], first[:, :, :], second[:, :, :], ALU.add).then_inc(chosen_done, 1)
                if part == 1:
                    dve.wait_ge(lge_done, q + 1)
                    dve.wait_ge(chosen_done, q + 1)
                    dve.tensor_tensor(gnum[:, :, :], chosen[:, :, :], lge[:, :, :], ALU.mult).then_inc(route, 1)
                    dve.tensor_reduce(top[:, 4, :], lge[:, :, :], X, ALU.add).then_inc(route, 1)
                    dve.wait_ge(route, base + 14)
                    dve.tensor_reduce(top[:, 5, :], gnum[:, :, :], X, ALU.add).then_inc(route, 1)
                    dve.reciprocal(top[:, 0, :], top[:, 4, :]).then_inc(route, 1)
                    dve.wait_ge(route, base + 16)
                    dve.tensor_tensor(tok_w[:, bass.ds(T * q, T)], top[:, 5, :], top[:, 0, :], ALU.mult).then_inc(route, 1)
                if part == 2:
                    dve.wait_ge(rank_done, q + 1)
                    dve.tensor_tensor(place[:, :, :], z_ps[:, T * E:2 * T * E].rearrange("p (t e) -> p t e", e=E),
                                      across(carry[:, :]), ALU.add).then_inc(route, 1)
                    dve.wait_ge(route, base + 18)
                    dve.tensor_tensor(carry[:, :], carry[:, :], z_ps[:, 2 * T * E:2 * T * E + E], ALU.add).then_inc(route, 1)
                    dve.tensor_tensor(place1[:, :, :], place[:, :, :], first[:, :, :], ALU.mult)
                    dve.tensor_tensor(place2[:, :, :], place[:, :, :], second[:, :, :], ALU.mult)
                    dve.tensor_scalar(token[:, :], token[:, :], float(S), None, ALU.add).then_inc(route, 1)
                    dve.wait_ge(route, base + 20)
                    dve.tensor_reduce(slot_f[:, :, 0], place1[:, :, :], X, ALU.add)
                    dve.tensor_reduce(slot_f[:, :, 1], place2[:, :, :], X, ALU.add).then_inc(slot_f_done, 1)
                    dve.tensor_copy(z[:, par, :, D:D + 1].bitcast(U32), token[:, :].unsqueeze(2))
                    dve.wait_ge(slot_f_done, q + 1)
                    dve.tensor_copy(slot[:, par, :, :], slot_f[:, :, :]).then_inc(slot_done, 1)

            def z_offset(b, t):
                offset(mv_z, rstd_z, off_z, z_rstd, z_off, t, T * b + t)

            def batch(b, h, par):
                next_h = h + par
                if not is_first(b):
                    z_step(T * b - 1, T - 1)
                    z_offset(b - 1, T - 1)
                for j in range(T):
                    n = T * b + j
                    dve.wait_ge(s_done, n + 1)
                    dve.tensor_reduce(neg_max[:, j:j + 1], s_ps[j % 2][:, :], X, ALU.max, negate=True).then_inc(max_done, 1)
                    if j:
                        row_sum(b, j - 1)
                    if j >= 2:
                        p_low(b, j - 2)
                    if not is_last(b):
                        if j < 2:
                            ln1_stat(b + 1, next_h, 1 - par, range(j * T // 2, (j + 1) * T // 2))
                        if j == 2:
                            ln1_moments(b + 1)
                        if j == 5:
                            ln1_offset(b + 1)
                row_sum(b, T - 1)
                p_low(b, T - 2)
                p_low(b, T - 1)
                if not is_first(b):
                    router(b - 1, 1 - par, 0)
                for t in range(1, T + 1):
                    c_step(T * b + t - 1, t - 1)
                    if t >= 2:
                        z_step(T * b + t - 2, t - 2)
                    if not is_last(b):
                        for u in Y_AHEAD.get(t, ()):
                            yT_low(b + 1, u)
                    offset(mv_c, rstd_c, off_c, c_rstd, c_off, t - 1, T * b + t - 1)
                    if t >= 2:
                        z_offset(b, t - 2)
                    if t <= 2 and not is_first(b):
                        router(b - 1, 1 - par, t)

            ln1_stat(0, 0, 0, range(T))
            ln1_moments(0)
            ln1_offset(0)
            for t in range(T):
                yT_low(0, t)
            dve.wait_ge(consts, NCONST)
            batches(dve, batch)
            z_step(NT - 1, T - 1)
            z_offset(B - 1, T - 1)
            for part in range(3):
                router(B - 1, 1, part)

            lists_at = tab["cnt"]
            dve.wait_ge(slot_done, B)
            dve.tensor_tensor(pad_f[:, :, :], carry[:, :].unsqueeze(2).broadcast_to([P, E, 2]),
                              lane[:, :].unsqueeze(1).broadcast_to([P, E, 2]), ALU.add).then_inc(tab_step, 1)
            dve.scalar_tensor_tensor(lists_at[:, :], rev[0:1, :], float(CAP), carry[0:1, :],
                                     ALU.mult, ALU.add).then_inc(tab_step, 1)
            dve.wait_ge(tab_step, 3)
            dve.tensor_copy(pad_at[:, :, :], pad_f[:, :, :]).then_inc(pads_at, 1)
            dve.tensor_scalar(tab_i[:, :], lists_at[:, :], float(SLOT - 1 - E * CAP), None, ALU.add).then_inc(tab_step, 1)
            dve.wait_ge(tab_step, 4)
            dve.tensor_scalar(tab_i2[:, :], tab_i[:, :], SLOT.bit_length() - 1, None, ALU.logical_shift_right).then_inc(tab_step, 1)
            dve.wait_ge(tab_step, 5)
            dve.tensor_copy(tab["tiles"][:, :], tab_i2[:, :]).then_inc(tab_step, 1)
            dve.wait_ge(tab_step, 6)
            dve.tensor_tensor_scan(tab["end"][:, :], tab["ones"][:, :], tab["tiles"][:, :], 0.0, ALU.mult, ALU.add).then_inc(tab_step, 1)
            dve.wait_ge(tab_step, 7)
            dve.tensor_tensor(tab_big[:, :, :], tab["g"][:, :].unsqueeze(2).broadcast_to([1, G, E]),
                              tab["end"][:, :].unsqueeze(1).broadcast_to([1, G, E]), ALU.is_ge).then_inc(tab_step, 1)
            dve.wait_ge(tab_step, 8)
            dve.tensor_reduce(tab_e[:, :], tab_big[:, :, :], X, ALU.add)
            dve.tensor_tensor(tab_big2[:, :, :], tab_big[:, :, :],
                              tab["tiles"][:, :].unsqueeze(1).broadcast_to([1, G, E]), ALU.mult).then_inc(tab_step, 1)
            dve.wait_ge(tab_step, 9)
            dve.tensor_reduce(tab_k[:, :], tab_big2[:, :, :], X, ALU.add).then_inc(tab_step, 1)
            dve.wait_ge(tab_step, 10)
            dve.tensor_tensor(tab_r[:, :], tab["g"][:, :], tab_k[:, :], ALU.subtract).then_inc(tab_step, 1)
            dve.tensor_scalar(tab_c[:, :], tab_e[:, :], float(CAP), None, ALU.mult).then_inc(tab_step, 1)
            dve.wait_ge(tab_step, 12)
            dve.scalar_tensor_tensor(tile_row[:, :], tab_r[:, :], float(SLOT), tab_c[:, :], ALU.mult, ALU.add)
            dve.tensor_scalar(tile_e[:, :], tab_e[:, :], float(E - 1), None, ALU.min).then_inc(tab_done, 1)

            for i in range(STAGES):
                e, lo, hi = i // 2, (w2_lo if i % 2 else w1_lo), (w2_hi if i % 2 else w1_hi)
                dve.wait_ge(whi_done, i + 1)
                dve.scalar_tensor_tensor(lo[:, e, :], stage[:, i % 4, :], WSCALE, hi[:, e, :],
                                         ALU.mult, ALU.subtract).then_inc(wlo_done, 1)
            dve.wait_ge(b_in, 32)
            dve.wait_ge(tab_done, 1)

            def slots_low(g, par):
                for c in range(2):
                    dve.wait_ge(shi_done, 2 * g + c + 1)
                    cols = slice(c * HALF, (c + 1) * HALF)
                    dve.tensor_tensor(s_lo[:, par, cols], tr_ps[c][:, :], s_hi[:, par, cols], ALU.subtract).then_inc(slo_done, 1)
                dve.tensor_copy(who_all[:, bass.ds(SH * g, SH)].unsqueeze(2), zin[:, par, :, D:D + 1].bitcast(U32)).then_inc(who_in, 1)

            def split_hidden(g, par):
                dve.wait_ge(gelu_done, MH * (g + 1))
                if not isinstance(g, int) or g >= 2:
                    dve.wait_ge(ye_done, SH * (g - 1))
                dve.tensor_copy(h_hi[:, par, :], h32[:, par, :]).then_inc(hhi_done, 1)
                dve.wait_ge(hhi_done, g + 1)
                dve.tensor_tensor(h_lo[:, par, :], h32[:, par, :], h_hi[:, par, :], ALU.subtract).then_inc(hlo_done, 1)

            def expert_out(g, par):
                at = dve.value_load(tile_e[0:1, bass.ds(g, 1)], min_val=0, max_val=E - 1) * D
                if not isinstance(g, int) or g >= 2:
                    dve.wait_ge(added, 16 * SH * (g - 1))
                dve.wait_ge(who_in, g + 1)
                dve.tensor_copy(who[:, par, :], who_all[:, bass.ds(SH * g, SH)]).then_inc(who_done, 1)
                for s in range(SH):
                    dve.wait_ge(ye_done, SH * g + s + 1)
                    dve.scalar_tensor_tensor(yo[:, par, s, :], y_ps[par][s][:, :], 1.0 / WSCALE,
                                             b2_all[:, bass.ds(at, D)], ALU.mult, ALU.add).then_inc(yo_done, 1)

            def step(s, par=None):
                par = s % 2 if par is None else par
                if not isinstance(s, int) or s + 1 < G:
                    slots_low(s + 1, 1 - par)
                if not isinstance(s, int) or s < G:
                    split_hidden(s, par)
                if not isinstance(s, int) or s >= 1:
                    expert_out(s - 1, 1 - par)
            slots_low(0, 0)
            expert_steps(dve, step)

            def final_stats(q, i, par):
                w = tok_w[:, bass.ds(QT * q, QT)]
                dve.wait_ge(fin_a_in[par], 16 * i + 16)
                for t in range(QT):
                    last = dve.bn_stats(st_f[:, par, t, :], fin_a[:, par, t, :])
                last.then_inc(f_stats, 1)
                dve.tensor_tensor(w_sq[:, par, :], w, w, ALU.mult).then_inc(f_sq, 1)
                dve.wait_ge(f_stats, q + 1)
                dve.nop(nofuse=True)
                for t in range(QT):
                    last = dve.bn_aggr(mv_f[:, par, t, :], st_f[:, par, t, :])
                last.then_inc(f_mv, 1)
                dve.wait_ge(f_mv, q + 1)
                dve.wait_ge(f_sq, q + 1)
                dve.tensor_tensor(var_f[:, par, :], mv_f[:, par, :, 1], w_sq[:, par, :], ALU.mult).then_inc(f_var, 1)
                dve.wait_ge(f_var, q + 1)
                dve.tensor_scalar(ve_f[:, par, :], var_f[:, par, :], EPS, None, ALU.add).then_inc(f_ve, 1)

            def final_offset(q, par):
                dve.wait_ge(f_rstd, q + 1)
                dve.tensor_tensor(mul_f[:, par, :], rstd_f[:, par, :], tok_w[:, bass.ds(QT * q, QT)], ALU.mult).then_inc(f_mul, 1)
                dve.wait_ge(f_mul, q + 1)
                dve.scalar_tensor_tensor(off_f[:, par, :], mv_f[:, par, :, 0], -1.0, mul_f[:, par, :],
                                         ALU.mult, ALU.mult).then_inc(f_off, 1)

            def final(i, par, end=False):
                q = FB * i + par
                if not end:
                    final_stats(q + 1, i + (par + 1) // FB, (par + 1) % FB)
                final_offset(q, par)
            final_stats(0, 0, 0)
            with dve.Fori(0, NF // FB - 1) as i:
                for par in range(FB):
                    final(i, par)
            for par in range(FB):
                final(NF // FB - 1, par, par == FB - 1)

        @block.tensor
        def _(pe):
            def transpose_y(q, par, t):
                n = T * q + t
                pe.wait_ge(y_done, n + 1)
                if t % 2 and not is_first(q):
                    pe.wait_ge(exp_done, T * q)
                if not isinstance(n, int) or n >= 2:
                    pe.wait_ge(yT_lo_done, n - 1)
                for k in range(KD):
                    last = pe.transpose(yt_ps[t % 2][:, k * P:(k + 1) * P], y[:, par, t, k * P:(k + 1) * P], ident[:, :])
                last.then_inc(yT_done, 1)

            def scores(b, j, between):
                n = T * b + j
                if j == 0:
                    pe.wait_ge(yT_lo_done, T * (b + 1))
                if not isinstance(n, int) or n >= 2:
                    pe.wait_ge(exp_done, n - 1)
                row = s_ps[j % 2]
                mine = slice(j * P, (j + 1) * P)
                chunks = [(max(j * P, c * HALF), (c + 1) * HALF) for c in range(2) if (c + 1) * HALF > j * P]
                for c, (lo, hi) in enumerate(chunks):
                    if c == len(chunks) - 1:
                        between()
                    for k in range(KD):
                        for i, (l, r) in enumerate(((yT_hi, yT_hi), (yT_hi, yT_lo), (yT_lo, yT_hi))):
                            last = pe.matmul(row[:, lo:hi], l[:, k, mine], r[:, k, lo:hi],
                                             start=(k == 0 and i == 0), stop=(k == KD - 1 and i == 2))
                if j:
                    pe.wait_ge(above_done, (T - 1) * b + j)
                for i in range(j):
                    last = pe.transpose(row[:, i * P:(i + 1) * P],
                                        above[i][:, (j - i - 1) * P:(j - i) * P], ident[:, :])
                last.then_inc(s_done, 1)

            def context(b, par, t, js):
                m = T * b + t
                if 0 in js and (not isinstance(m, int) or m >= 2):
                    pe.wait_ge(ctxn_done, m - 1)
                rows = slice(t * P, (t + 1) * P)
                for j in js:
                    if t < 2:
                        pe.wait_ge(plo_done, T * b + j + 1)
                        pe.wait_ge(ylo_done, T * b + j + 1)
                    for i, (l, r) in enumerate(((p_hi, y_hi[:, par]), (p_hi, y_lo), (p_lo, y_hi[:, par]))):
                        last = pe.matmul(c_ps[t % 2][:, :], l[:, j, rows], r[:, j, :],
                                         start=(j == 0 and i == 0), stop=(j == T - 1 and i == 2))
                if T - 1 in js:
                    last.then_inc(pv_done, 1)

            def transpose_z(q, par, t):
                m = T * q + t
                pe.wait_ge(z_done, m + 1)
                if not isinstance(m, int) or m:
                    pe.wait_ge(lgT_done, m)
                if t == 0 and not is_first(q):
                    pe.wait_ge(slot_done, q)
                for k in range(KD):
                    last = pe.transpose(z_ps[:, k * P:(k + 1) * P], z[:, par, t, k * P:(k + 1) * P], ident[:, :])
                last.then_inc(ztr_done, 1)

            def logits(q, t):
                pe.wait_ge(zT_done, T * q + t + 1)
                for k in range(KD):
                    last = pe.matmul(z_ps[0:E, 0:P], gate[:, k, :], zT[:, k * P:(k + 1) * P],
                                     start=(k == 0), stop=(k == KD - 1))
                last.then_inc(gate_done, 1)

            def logits_back(q):
                pe.wait_ge(lgT_done, T * (q + 1))
                pe.nop(nofuse=True)
                for t in range(T):
                    last = pe.transpose(z_ps[:, t * E:(t + 1) * E], lgT[:, t * P:(t + 1) * P], ident[0:E, 0:E])
                last.then_inc(lg_ready, 1)

            def ranks(q):
                pe.wait_ge(chosen_done, q + 1)
                flat = chosen[:, :, :].rearrange("p t e -> p (t e)")
                W = T * E
                pe.matmul(z_ps[:, W:2 * W], before[:, :], flat, start=True, stop=False, skip_group_check=True)
                for s in range(1, T):
                    pe.matmul(z_ps[:, W + s * E:2 * W], ones[:, :], flat[:, 0:W - s * E], start=False,
                              stop=(s == T - 1), skip_group_check=True)
                for s in range(T):
                    last = pe.matmul(z_ps[:, 2 * W:2 * W + E], ones[:, :], flat[:, s * E:(s + 1) * E],
                                     start=(s == 0), stop=(s == T - 1), skip_group_check=True)
                last.then_inc(rank_done, 1)

            def batch(b, h, par):
                for j in range(T):
                    late = not is_first(b) and j < 3
                    scores(b, j, (lambda: transpose_z(b - 1, 1 - par, T - 3 + j)) if late else (lambda: None))
                    if late:
                        logits(b - 1, T - 3 + j)
                    if j == 4 and not is_first(b):
                        logits_back(b - 1)
                context(b, par, 0, range(T - 1))
                context(b, par, 1, range(T // 2))
                context(b, par, 0, [T - 1])
                context(b, par, 1, range(T // 2, T))
                if not is_first(b):
                    ranks(b - 1)
                for t in range(2, T):
                    if not is_last(b):
                        for u in Y_AHEAD[t]:
                            transpose_y(b + 1, 1 - par, u)
                    context(b, par, t, range(T // 2))
                    if t >= 3:
                        transpose_z(b, par, t - 3)
                    context(b, par, t, range(T // 2, T))
                    if t >= 3:
                        logits(b, t - 3)

            pe.wait_ge(consts, NCONST)
            pe.wait_ge(dve_consts, 2)
            pe.wait_ge(const_dma, 16)
            for t in range(T):
                transpose_y(0, 0, t)
            batches(pe, batch)
            for t in range(T - 3, T):
                transpose_z(B - 1, 1, t)
                logits(B - 1, t)
            logits_back(B - 1)
            ranks(B - 1)

            pe.wait_ge(wlo_done, STAGES)
            pe.wait_ge(tab_done, 1)
            pe.wait_ge(rank_done, B)
            pe.wait_ge(slot_done, B)

            def transpose_slots(g, par):
                odd = g % 2 if isinstance(g, int) else par
                count = (g // 2 + 1) * 16 if isinstance(g, int) else 8 * (g - par) + 16
                pe.wait_ge(zin_in[odd], count)
                for c in range(2):
                    if not isinstance(g, int) or g:
                        pe.wait_ge(slo_done, 2 * g - 1 + c)
                    for kk in range(2):
                        k = 2 * c + kk
                        for s in range(SH):
                            at = kk * SLOT + s * P
                            last = pe.transpose(tr_ps[c][:, at:at + P], zin[:, par, s, k * P:(k + 1) * P], ident[:, :])
                    last.then_inc(tr_done, 1)

            def up(g, par):
                e = pe.value_load(tile_e[0:1, bass.ds(g, 1)], min_val=0, max_val=E - 1)
                pe.wait_ge(slo_done, 2 * g + 2)
                if not isinstance(g, int) or g >= 2:
                    pe.wait_ge(gelu_done, MH * (g - 1))
                for m in range(MH):
                    for k in range(KD):
                        cols = slice(k * H + m * P, k * H + (m + 1) * P)
                        hi = w1_hi[:, bass.ds(e, 1), cols].rearrange("p e c -> p (e c)")
                        lo = w1_lo[:, bass.ds(e, 1), cols].rearrange("p e c -> p (e c)")
                        rows = slice(k * SLOT, (k + 1) * SLOT)
                        for i, (l, r) in enumerate(((hi, s_hi), (hi, s_lo), (lo, s_hi))):
                            last = pe.matmul(h_ps[par][:, m * SLOT:(m + 1) * SLOT], l, r[:, par, rows],
                                             start=(k == 0 and i == 0), stop=(k == KD - 1 and i == 2))
                last.then_inc(h_done, 1)

            def down(g, par):
                e = pe.value_load(tile_e[0:1, bass.ds(g, 1)], min_val=0, max_val=E - 1)
                pe.wait_ge(hlo_done, g + 1)
                for s in range(SH):
                    if not isinstance(g, int) or g >= 2:
                        pe.wait_ge(yo_done, SH * (g - 2) + s + 1)
                    for m in range(MH):
                        hi = w2_hi[:, bass.ds(e, 1), m * D:(m + 1) * D].rearrange("p e c -> p (e c)")
                        lo = w2_lo[:, bass.ds(e, 1), m * D:(m + 1) * D].rearrange("p e c -> p (e c)")
                        cols = slice(m * SLOT + s * P, m * SLOT + (s + 1) * P)
                        for i, (l, r) in enumerate(((h_hi, hi), (h_hi, lo), (h_lo, hi))):
                            last = pe.matmul(y_ps[par][s][:, :], l[:, par, cols], r,
                                             start=(m == 0 and i == 0), stop=(m == MH - 1 and i == 2))
                    last.then_inc(ye_done, 1)

            def step(s, par=None):
                par = s % 2 if par is None else par
                if not isinstance(s, int) or s + 1 < G:
                    transpose_slots(s + 1, 1 - par)
                if not isinstance(s, int) or s < G:
                    up(s, par)
                if not isinstance(s, int) or s >= 1:
                    down(s - 1, 1 - par)
            transpose_slots(0, 0)
            expert_steps(pe, step)


_INS = ["L0_attn_x", "L0_ffn_gate_w", "L0_ffn_w1", "L0_ffn_b1", "L0_ffn_w2", "L0_ffn_b2"]


def kernel(**inputs):
    import numpy as _np
    import concourse.bacc as _bacc
    from concourse.bass_utils import run_bass_kernel_spmd as _run

    nc = _bacc.Bacc("TRN2", target_bir_lowering=False, num_devices=1)
    arrays, args = {}, []
    for name in _INS:
        a = _np.ascontiguousarray(inputs[name])
        arrays[f"in_{name}"] = a
        args.append(nc.dram_tensor(f"in_{name}", a.shape, mybir.dt.from_np(a.dtype), kind="ExternalInput").ap())
    result = nc.dram_tensor("out_0", inputs["L0_attn_x"].shape, F32, kind="ExternalOutput").ap()
    attention_then_experts(nc, *args, result)
    r = _run(nc, [arrays], core_ids=[0])
    return r.results[0]["out_0"]
```

```python
from contextlib import ExitStack

import numpy as np

import concourse.bass as bass
from concourse import mybir

F32 = mybir.dt.float32
F16 = mybir.dt.float16
U32 = mybir.dt.uint32
I32 = mybir.dt.int32
ALU = mybir.AluOpType
ACT = mybir.ActivationFunctionType
X = mybir.AxisListType.X

P = 128
SLOT = 256
EPS = 1e-5
PSCALE = 1024.0
WSCALE = 64.0
FAR = -1e30


def attention_then_experts(nc, x, gate_w, w1, b1, w2, b2, out):
    B, S, D = x.shape
    E, _, H = w1.shape
    T = S // P
    KD = D // P
    MH = H // P
    NTOK = B * S
    NT = B * T
    CAP = NTOK + SLOT
    G = 2 * NTOK // SLOT + E - 1
    ROW = D + 8
    HALF = 512
    assert T == 8 and KD == 4 and S == 2 * HALF and D == HALF and MH == 2 and G % 2 == 1 and B % 2 == 0 and B >= 6

    x_v = x.rearrange("b (t p) d -> b p t d", p=P)
    xt_v = x.rearrange("b (t p) d -> (b t) p d", p=P)
    out_v = out.rearrange("b (t p) d -> p (b t) d", p=P)
    lists = nc.dram_tensor("slot_lists", (E * CAP + (E - 1) * SLOT, ROW), F32, kind="Internal").ap()
    acc = nc.dram_tensor("expert_sum", (NTOK + SLOT, D), F32, kind="Internal").ap()
    mid = nc.dram_tensor("after_attention", (NTOK, D), F32, kind="Internal").ap()
    mid_t = mid.rearrange("(n p) d -> n p d", p=P)
    mid_v = mid.rearrange("(n p) d -> p n d", p=P)
    acc_t = acc.rearrange("(n p) d -> n p d", p=P)
    acc_v = acc.rearrange("(n p) d -> p n d", p=P)

    with ExitStack() as ctx:
        def sem(name):
            return ctx.enter_context(nc.semaphore(name))

        def sb(name, shape, dt, where=ctx):
            return where.enter_context(nc.sbuf_tensor(name, shape, dt))

        def bank(name, where=ctx, shape=(P, HALF)):
            return where.enter_context(nc.psum_tensor(name, list(shape), F32))

        ident = sb("ident", [P, P], F32)
        before = sb("before", [P, P], F16)
        ones = sb("ones", [P, P], F16)
        warm = sb("warm", [1, 1], F32)
        pow_exp = sb("pow_exp", [P, T], F32)
        rev = sb("rev", [P, E], F32)
        gate = sb("gate", [P, KD, E], F32)
        gate_hl = sb("gate_hl", [P, KD, 2, E], F16)
        b1_col = sb("b1_col", [P, E * MH], F32)
        tok_w = sb("tok_w", [P, NT], F32)
        pad = sb("pad", [P, 2, ROW], F32)
        token = sb("token", [P, T], F32)
        carry = sb("carry", [P, E], F32)
        lg_parts = sb("lg_parts", [P, T, 2, E], F32)
        lg = sb("lg", [P, T, E], F32)
        lg2 = sb("lg2", [P, T, E], F32)
        lgd = sb("lgd", [P, T, E], F32)
        lge = sb("lge", [P, T, E], F32)
        eq = sb("eq", [P, T, E], F32)
        first = sb("first", [P, T, E], F32)
        second = sb("second", [P, T, E], F32)
        chosen = sb("chosen", [P, T, E], F16)
        gnum = sb("gnum", [P, T, E], F32)
        place = sb("place", [P, T, E], F32)
        place1 = sb("place1", [P, T, E], F32)
        place2 = sb("place2", [P, T, E], F32)
        top = sb("top", [P, 6, T], F32)
        slot_f = sb("slot_f", [P, T, 2], F32)
        slot = sb("slot", [P, 2, T, 2], U32)
        pad_row = sb("pad_row", [1, E], I32)
        st_x = sb("st_x", [P, T, 6], F32)
        mv_x = sb("mv_x", [P, T, 2], F32)
        var_x = sb("var_x", [P, T], F32)
        rstd_x = sb("rstd_x", [P, T], F32)
        off_x = sb("off_x", [P, T], F32)
        st_c = sb("st_c", [P, T, 6], F32)
        mv_c = sb("mv_c", [P, T, 2], F32)
        var_c = sb("var_c", [P, T], F32)
        rstd_c = sb("rstd_c", [P, T], F32)
        off_c = sb("off_c", [P, T], F32)
        st_z = sb("st_z", [P, T, 6], F32)
        mv_z = sb("mv_z", [P, T, 2], F32)
        var_z = sb("var_z", [P, T], F32)
        rstd_z = sb("rstd_z", [P, T], F32)
        off_z = sb("off_z", [P, T], F32)
        neg_max = sb("neg_max", [P, T], F32)
        psum_row = sb("psum_row", [P, T], F32)
        psum_sc = sb("psum_sc", [P, T], F32)
        pinv = sb("pinv", [P, T], F32)
        V = 2 * E
        lens = sb("lens", [1, E], I32)
        halves_i = sb("halves_i", [1, 2, E], I32)
        halves = sb("halves", [1, 2, E], F32)
        v_tiles = sb("v_tiles", [1, V], F32)
        v_ones = sb("v_ones", [1, V], F32)
        v_end = sb("v_end", [1, V], F32)
        v_base = sb("v_base", [1, V + 1], F32)
        v_step = sb("v_step", [1, V], F32)
        v_jump = sb("v_jump", [1, V], F32)
        v_next = sb("v_next", [1, V], F32)
        tab_g = sb("tab_g", [1, G], F32)
        tab_e = sb("tab_e", [1, G], F32)
        tab_r = sb("tab_r", [1, G], F32)
        tile_row = sb("tile_row", [1, G], I32)
        tile_e = sb("tile_e", [1, G], I32)

        CUT = T // 2
        QT = 4
        FB = 8
        EARLY = FB * QT
        assert EARLY <= (G - 3) // 2
        st_f = sb("st_f", [P, FB, QT, 6], F32)
        mv_f = sb("mv_f", [P, FB, QT, 2], F32)
        w_sq = sb("w_sq", [P, FB, QT], F32)
        var_f = sb("var_f", [P, FB, QT], F32)
        ve_f = sb("ve_f", [P, FB, QT], F32)
        rstd_f = sb("rstd_f", [P, FB, QT], F32)
        mul_f = sb("mul_f", [P, FB, QT], F32)
        off_f = sb("off_f", [P, FB, QT], F32)

        with ExitStack() as a:
            y = sb("y", [P, 2, T, D], F32, a)
            yT_hi = sb("yT_hi", [P, KD, S], F16, a)
            yT_lo = sb("yT_lo", [P, KD, S], F16, a)
            above = [sb(f"above{j}", [P, S - P * (j + 1)], F32, a) for j in range(T - 1)]
            p32 = sb("p32", [P, 3, S], F32, a)
            y_hi = sb("y_hi", [P, 2, T, D], F16, a)
            y_lo = sb("y_lo", [P, T, D], F16, a)
            p_hi = sb("p_hi", [P, T, S], F16, a)
            p_lo = sb("p_lo", [P, T, S], F16, a)
            z = sb("z", [P, 2, T, ROW], F32, a)
            ctxn = sb("ctxn", [P, 2, D], F32, a)
            xres = sb("xres", [P, 2, D], F32, a)
            x1 = sb("x1", [P, 2, D], F32, a)
            zT_hi = sb("zT_hi", [P, 3, D], F16, a)
            zT_lo = sb("zT_lo", [P, 3, D], F16, a)
        with ExitStack() as a:
            w1_hi = sb("w1_hi", [P, E, KD * H], F16, a)
            w1_lo = sb("w1_lo", [P, E, KD * H], F16, a)
            w2_hi = sb("w2_hi", [P, E, MH * D], F16, a)
            w2_lo = sb("w2_lo", [P, E, MH * D], F16, a)
            with ExitStack() as c:
                stage = sb("stage", [P, 4, KD * H], F32, c)
                passed = sb("passed", [1, G, V], F32, c)
                passed_row = sb("passed_row", [1, G, V], F32, c)
                passed_e = sb("passed_e", [1, G, V], F32, c)
            fin_x = sb("fin_x", [P, FB, QT, D], F32, a)
            b2_all = sb("b2_all", [P, E * D], F32, a)
            zin = sb("zin", [P, 2, 2, ROW], F32, a)
            s_hi = sb("s_hi", [P, 2, KD * SLOT], F16, a)
            s_lo = sb("s_lo", [P, 2, KD * SLOT], F16, a)
            h32 = sb("h32", [P, 2, MH * SLOT], F32, a)
            h_hi = sb("h_hi", [P, 2, MH * SLOT], F16, a)
            h_lo = sb("h_lo", [P, 2, MH * SLOT], F16, a)
            yo = sb("yo", [P, 2, 2, D], F32, a)
            who_all = sb("who_all", [P, 2 * G], U32, a)
            who = sb("who", [P, 2, 2], U32, a)
        with ExitStack() as a:
            fin_a = sb("fin_a", [P, FB, QT, D], F32, a)

        with ExitStack() as a:
            s_ps = [bank(f"s_ps{i}", a, (P, S)) for i in range(2)]
            c_ps = [bank(f"c_ps{i}", a) for i in range(2)]
            t_ps = bank("t_ps", a)
            z_ps = bank("z_ps", a)
            yt_ps = [t_ps[:, :], s_ps[1][:, HALF:S]]
            zt_ps = [z_ps[:, :], s_ps[0][:, 0:HALF], s_ps[0][:, HALF:S]]
        with ExitStack() as a:
            tr_ps = [bank(f"tr_ps{i}", a) for i in range(2)]
            h_ps = [bank(f"h_ps{i}", a) for i in range(2)]
            y_ps = [[bank(f"y_ps{i}{s}", a) for s in range(2)] for i in range(2)]

        consts = sem("consts")
        dve_consts = sem("dve_consts")
        const_dma = sem("const_dma")
        x_first = [sem(f"x_first{i}") for i in range(T // 2)]
        x_in = [sem(f"x_in{i}") for i in range(2)]
        xres_in = [sem(f"xres_in{i}") for i in range(2)]
        mid_out = [sem(f"mid_out{i}") for i in range(2)]
        zero_out = sem("zero_out")
        warm_done, gate_sums = sem("warm_done"), sem("gate_sums")
        ln1_stats, ln1_mv, ln1_var, ln1_rstd, ln1_off = (sem(f"ln1_{n}") for n in ("stats", "mv", "var", "rstd", "off"))
        y_done = sem("y_done")
        yT_done, yT_hi_done, yT_lo_done = sem("yT_done"), sem("yT_hi_done"), sem("yT_lo_done")
        yhi_done, ylo_done = sem("yhi_done"), sem("ylo_done")
        s_done, above_done, exp_done = sem("s_done"), sem("above_done"), sem("exp_done")
        max_done, sum_done, inv_done = sem("max_done"), sem("sum_done"), sem("inv_done")
        phi_done, plo_done, pv_done = sem("phi_done"), sem("plo_done"), sem("pv_done")
        c_stats, c_mv, c_var, c_rstd, c_off = (sem(f"c_{n}") for n in ("stats", "mv", "var", "rstd", "off"))
        z_stats, z_mv, z_var, z_rstd, z_off = (sem(f"z_{n}") for n in ("stats", "mv", "var", "rstd", "off"))
        ctxn_done, x1_done, z_done = sem("ctxn_done"), sem("x1_done"), sem("z_done")
        ztr_done, zT_hi_done, zT_lo_done = sem("ztr_done"), sem("zT_hi_done"), sem("zT_lo_done")
        gate_hi_done, gate_lo_done, gate_done, lg_done = (sem("gate_hi_done"), sem("gate_lo_done"),
                                                          sem("gate_done"), sem("lg_done"))
        lgd_done, lge_done = sem("lgd_done"), sem("lge_done")
        route, chosen_done, rank_done, slot_done = sem("route"), sem("chosen_done"), sem("rank_done"), sem("slot_done")
        scat = [[sem(f"scat{i}_{t}") for t in range(T)] for i in range(2)]
        slot_f_done, token_done = sem("slot_f_done"), sem("token_done")
        pads_at, pads_out, tab_step, tab_done = sem("pads_at"), sem("pads_out"), sem("tab_step"), sem("tab_done")
        w_in = [sem(f"w_in{i}") for i in range(4)]
        whi_done, wlo_done, b_in = sem("whi_done"), sem("wlo_done"), sem("b_in")
        zin_in = [sem(f"zin_in{i}") for i in range(2)]
        tr_done, shi_done, slo_done = sem("tr_done"), sem("shi_done"), sem("slo_done")
        who_in, who_done = sem("who_in"), sem("who_done")
        h_done, gelu_done, hhi_done, hlo_done = sem("h_done"), sem("gelu_done"), sem("hhi_done"), sem("hlo_done")
        ye_done, yo_done = sem("ye_done"), sem("yo_done")
        added = sem("added")
        fin_a_in = [sem(f"fin_a_in{i}") for i in range(FB)]
        fin_x_in = [sem(f"fin_x_in{i}") for i in range(FB)]
        early_in = sem("early_in")
        f_stats, f_mv, f_sq, f_var, f_ve, f_rstd, f_mul, f_off = (
            sem(f"f_{n}") for n in ("stats", "mv", "sq", "var", "ve", "rstd", "mul", "off"))
        f_norm, f_sum = sem("f_norm"), sem("f_sum")
        fin_out = [sem(f"fin_out{i}") for i in range(FB)]

        NCONST = 11
        ROUTE = 15
        TAB = 9
        SH = SLOT // P
        STAGES = 2 * E
        SPLIT = 2
        UNDER = SPLIT * (T - 3)

        def split_under(t):
            return range(SPLIT * (t - 2), SPLIT * (t - 1)) if 2 <= t <= T - 2 else ()
        NF = NT // QT
        assert NF == 2 * FB

        def batches(eng, one):
            one(0, 0, 0)
            one(1, 0, 1)
            with eng.Fori(1, B // 2 - 1) as h:
                one(2 * h, h, 0)
                one(2 * h + 1, h, 1)
            one(B - 2, B // 2 - 1, 0)
            one(B - 1, B // 2 - 1, 1)

        def is_first(b):
            return isinstance(b, int) and b == 0

        def is_last(b):
            return isinstance(b, int) and b == B - 1

        Y_AHEAD = {2: (0, 1), 3: (2,), 4: (3,), 5: (4,), 6: (5,), 7: (6, 7)}

        def expert_steps(eng, one):
            for s in range(3):
                one(s)
            with eng.Fori(0, (G - 5) // 2) as i:
                one(2 * i + 3, 1)
                one(2 * i + 4, 0)
            for s in range(G - 2, G + 1):
                one(s)

        block = ctx.enter_context(nc.Block())

        @block.sync
        def _(sp):
            for i in range(T // 2):
                sp.dma_start(y[:, 0, 2 * i:2 * i + 2, :], x_v[0][:, 2 * i:2 * i + 2, :]).then_inc(x_first[i], 16)
            sp.dma_start(gate[:, :, :], gate_w.rearrange("(k p) e -> p k e", p=P)).then_inc(const_dma, 16)
            sp.dma_start(b1_col[:, :], b1.rearrange("e (m p) -> p (e m)", p=P),
                         allow_slow_non_contiguous=True).then_inc(b_in, 16)
            for i in range(2):
                sp.dma_start(xres[:, i, :], xt_v[i]).then_inc(xres_in[i], 16)
            sp.dma_start(y[:, 1, :, :], x_v[1]).then_inc(x_in[1], 16)
            sp.wait_ge(consts, NCONST)
            for n in range(NTOK // P + SH):
                sp.dma_start(acc_t[n], pad[:, 0, 0:D]).then_inc(zero_out, 16)
            for n in range(E - 1):
                at = E * CAP + n * SLOT
                sp.dma_start(lists[at:at + SLOT, :].rearrange("(s p) r -> p s r", p=P),
                             pad[:, :, :]).then_inc(zero_out, 16)

            def load_weights(i):
                if i >= 4:
                    sp.wait_ge(wlo_done, i - 3)
                e, second_w = i // 2, i % 2
                src = (w2[e].rearrange("(m p) d -> p m d", p=P) if second_w
                       else w1[e].rearrange("(k p) h -> p k h", p=P))
                sp.dma_start(stage[:, i % 4, :].rearrange("p (k h) -> p k h", k=MH if second_w else KD),
                             src).then_inc(w_in[i % 4], 16)

            def batch(b, h, par):
                last = is_last(b)
                if not (isinstance(b, int) and b >= B - 2):
                    sp.wait_ge(yT_done, T * (b + 1))
                    sp.wait_ge(ylo_done, T * (b + 1))
                    sp.dma_start(y[:, par, :, :], x_v[bass.ds(b + 2, 1)].rearrange("b p t d -> p (b t) d")
                                 ).then_inc(x_in[par], 16)
                if last:
                    sp.wait_ge(plo_done, NT)
                    sp.wait_ge(ylo_done, NT)
                    for i in range(4):
                        load_weights(i)
                for t in range(T):
                    m = T * b + t
                    if last and 2 <= t <= T - 2:
                        for i in range(SPLIT * t, SPLIT * (t + 1)):
                            load_weights(i)
                    sp.wait_ge(x1_done, m + 1)
                    sp.dma_start(mid_t[bass.ds(m, 1)].rearrange("n p d -> p (n d)"),
                                 x1[:, t % 2, :]).then_inc(mid_out[t % 2], 16)
                    if not (last and t >= T - 2):
                        sp.dma_start(xres[:, t % 2, :], xt_v[bass.ds(m + 2, 1)].rearrange("n p d -> p (n d)")
                                     ).then_inc(xres_in[t % 2], 16)
            batches(sp, batch)

            sp.wait_ge(pv_done, NT)
            for t in range(T):
                sp.wait_ge(scat[0][t], 32 * B // 2)
            sp.dma_start(b2_all[:, :], b2.rearrange("e d -> (e d)").partition_broadcast(P)).then_inc(b_in, 16)
            for i in range(UNDER + 4, STAGES):
                load_weights(i)

            sp.wait_ge(pads_at, 1)

            def write_pad(e):
                row = sp.value_load(pad_row[0:1, e:e + 1], min_val=e * CAP, max_val=e * CAP + NTOK)
                sp.dma_start(lists[bass.ds(row, SLOT), :].rearrange("(s p) r -> p s r", p=P),
                             pad[:, :, :]).then_inc(pads_out, 16)

            for i in range(2):
                sp.wait_ge(mid_out[i], 16 * NT // 2)
            for par in range(2):
                for t in range(T):
                    sp.wait_ge(scat[par][t], 32 * B // 2)
            sp.wait_ge(zero_out, 16 * (NTOK // P + SH + E - 1))
            sp.wait_ge(tab_done, 1)
            def load_slots(g, par):
                if not isinstance(g, int) or g >= 2:
                    sp.wait_ge(tr_done, 2 * (g - 1))
                    sp.wait_ge(who_in, g - 1)
                row = sp.value_load(tile_row[0:1, bass.ds(g, 1)], min_val=0,
                                    max_val=E * CAP + (E - 2) * SLOT)
                sp.dma_start(zin[:, par, :, :], lists[bass.ds(row, SLOT), :].rearrange("(s p) r -> p s r", p=P)
                             ).then_inc(zin_in[par], 16)
            load_slots(0, 0)
            load_slots(1, 1)
            sp.wait_ge(wlo_done, STAGES)
            fin_x_tiles = fin_x[:, :, :, :].rearrange("p b t d -> p (b t) d")

            def load_pair(i):
                load_slots(2 * i + 2, 0)
                load_slots(2 * i + 3, 1)
                sp.dma_start(fin_x_tiles[:, bass.ds(i, 1), :], mid_v[:, bass.ds(i, 1), :]).then_inc(early_in, 16)

            WHOLE = 2 * NTOK // SLOT - E
            assert 2 * (E // 2) + 2 <= WHOLE
            for i in range(E // 2):
                load_pair(i)
                write_pad(2 * i)
                write_pad(2 * i + 1)
            sp.wait_ge(pads_out, 16 * E)
            with sp.Fori(E // 2, EARLY) as i:
                load_pair(i)
            for g in range(2 * EARLY + 2, G):
                load_slots(g, g % 2)

            def load_residual(i, par):
                sp.dma_start(fin_x[:, par, :, :], mid_v[:, bass.ds(QT * (FB * i + par), QT), :]).then_inc(fin_x_in[par], 16)

            def load_sums(i, par):
                sp.dma_start(fin_a[:, par, :, :], acc_v[:, bass.ds(QT * (FB * i + par), QT), :]).then_inc(fin_a_in[par], 16)

            sp.wait_ge(added, 16 * SH * G)
            sp.wait_ge(ye_done, SH * G)
            for par in range(FB):
                load_sums(0, par)
            for par in range(FB):
                sp.wait_ge(fin_out[par], 16)
                load_sums(1, par)
                load_residual(1, par)
            for par in range(FB):
                sp.wait_ge(fin_out[par], 16 * NF // FB)

        @block.gpsimd
        def _(pool):
            pool.memset(ident[:, :], 0.0).then_inc(consts, 1)
            pool.memset(before[:, :], 1.0).then_inc(consts, 1)
            pool.memset(pow_exp[:, :], -0.5).then_inc(consts, 1)
            pool.memset(z[:, :, :, :], 0.0).then_inc(consts, 1)
            pool.memset(pad[:, :, :], 0.0).then_inc(consts, 1)
            pool.wait_ge(consts, 5)
            pool.affine_select(out=ident[:, :], in_=ident[:, :], compare_op=ALU.not_equal, fill=1.0,
                               base=0, pattern=[[-1, P]], channel_multiplier=1).then_inc(consts, 1)
            pool.affine_select(out=before[:, :], in_=before[:, :], compare_op=ALU.is_gt, fill=0.0,
                               base=0, pattern=[[1, P]], channel_multiplier=-1).then_inc(consts, 1)
            pool.iota(token[:, :], pattern=[[P, T]], base=-S, channel_multiplier=1,
                      allow_small_or_imprecise_dtypes=True).then_inc(consts, 1)
            pool.iota(carry[:, :], pattern=[[CAP, E]], base=0, channel_multiplier=0,
                      allow_small_or_imprecise_dtypes=True).then_inc(consts, 1)
            pool.iota(rev[:, :], pattern=[[-1, E]], base=E, channel_multiplier=0,
                      allow_small_or_imprecise_dtypes=True).then_inc(consts, 1)
            pool.iota(pad[:, :, D:D + 1].bitcast(U32).rearrange("p s r -> p (s r)"), pattern=[[P, 2]], base=NTOK,
                      channel_multiplier=1).then_inc(consts, 1)
            pool.iota(tab_g[:, :], pattern=[[1, G]], base=0, channel_multiplier=0,
                      allow_small_or_imprecise_dtypes=True).then_inc(tab_step, 1)

            def power(out, in_, wait, n, done):
                pool.wait_ge(wait, n)
                pool.tensor_tensor(out, in_, pow_exp[:, 0:in_.shape[1]], ALU.pow).then_inc(done, 1)

            def scatter(n, par, t):
                pool.wait_ge(slot_done, n + 1)
                pool.nop(nofuse=True)
                for k in range(2):
                    pool.indirect_dma_start(out=lists, in_=z[:, par, t, :], in_offset=None,
                                            out_offset=bass.IndirectOffsetOnAxis(ap=slot[:, par, t, k:k + 1], axis=0)
                                            ).then_inc(scat[par][t], 16)

            SEND = {2: (0,), 3: (1, 2), 4: (3,), 5: (4, 5), 6: (6, 7)}

            def batch(b, h, par):
                for j in range(T):
                    if not is_first(b):
                        pool.wait_ge(pv_done, T * b)
                    pool.wait_ge(yhi_done, T * b + j + 1)
                    pool.tensor_tensor(y_lo[:, j, :], y[:, par, j, :], y_hi[:, par, j, :], ALU.subtract).then_inc(ylo_done, 1)
                if not is_last(b):
                    power(rstd_x[:, :], var_x[:, :], ln1_var, b + 2, ln1_rstd)
                for t in range(T):
                    m = T * b + t
                    power(rstd_c[:, t:t + 1], var_c[:, t:t + 1], c_var, m + 1, c_rstd)
                    if t:
                        power(rstd_z[:, t - 1:t], var_z[:, t - 1:t], z_var, m, z_rstd)
                    pool.wait_ge(ctxn_done, m + 1)
                    half_batch = T // 2
                    pool.wait_ge(xres_in[t % 2], 16 * (half_batch * b + t // 2 + 1))
                    if t >= 2 or not is_first(b):
                        pool.wait_ge(mid_out[t % 2], 16 * (half_batch * b + t // 2))
                        pool.wait_ge(z_done, m - 1)
                    pool.tensor_tensor(x1[:, t % 2, :], xres[:, t % 2, :], ctxn[:, t % 2, :], ALU.add).then_inc(x1_done, 1)
                    if t == T - 1:
                        if is_last(b):
                            scatter(b - 1, 1 - par, T - 1)
                        power(rstd_z[:, t:t + 1], var_z[:, t:t + 1], z_var, m + 1, z_rstd)
                    if not is_first(b):
                        for u in SEND.get(t, ()):
                            if not (is_last(b) and u == T - 1):
                                scatter(b - 1, 1 - par, u)

            power(rstd_x[:, :], var_x[:, :], ln1_var, 1, ln1_rstd)
            batches(pool, batch)
            for t in range(T):
                scatter(B - 1 if t < CUT else B, 1, t)
            def add_rows(g, par):
                pool.wait_ge(who_done, g + 1)
                for s in range(SH):
                    pool.wait_ge(yo_done, SH * g + s + 1)
                    if s == 0 and (not isinstance(g, int) or g):
                        pool.wait_ge(added, 16 * SH * g)
                    pool.nop(nofuse=True)
                    pool.indirect_dma_start(out=acc, in_=yo[:, par, s, :], in_offset=None, compute_op=ALU.add,
                                            out_offset=bass.IndirectOffsetOnAxis(ap=who[:, par, s:s + 1], axis=0)
                                            ).then_inc(added, 16)
            pool.wait_ge(zero_out, 16 * (NTOK // P + SH + E - 1))
            add_rows(0, 0)
            with pool.Fori(0, (G - 3) // 2) as i:
                add_rows(2 * i + 1, 1)
                add_rows(2 * i + 2, 0)
            add_rows(G - 2, 1)
            add_rows(G - 1, 0)

            def final_power(q, par):
                pool.wait_ge(f_ve, q + 1)
                pool.tensor_tensor(rstd_f[:, par, :], ve_f[:, par, :], pow_exp[:, 0:QT], ALU.pow).then_inc(f_rstd, 1)

            def final_add(q, i, par, early):
                if early:
                    pool.wait_ge(early_in, 16 * EARLY)
                else:
                    pool.wait_ge(fin_x_in[par], 16 * i)
                pool.wait_ge(f_norm, QT * (q + 1))
                pool.tensor_tensor(fin_x[:, par, :, :], fin_x[:, par, :, :], fin_a[:, par, :, :], ALU.add).then_inc(f_sum, 1)

            def final(i, par, end=False):
                q = FB * i + par
                if not end:
                    final_power(q + 1, (par + 1) % FB)
                final_add(q, i, par, isinstance(i, int) and i == 0)
            final_power(0, 0)
            for par in range(FB):
                final(0, par)
            for par in range(FB):
                final(1, par, par == FB - 1)

        @block.scalar
        def _(act):
            def norm_x(q, par, t):
                act.wait_ge(ln1_off, q + 1)
                act.activation(y[:, par, t, :], y[:, par, t, :], ACT.Identity, bias=off_x[:, t:t + 1],
                               scale=rstd_x[:, t:t + 1]).then_inc(y_done, 1)

            def y_high(q, par, t):
                act.wait_ge(y_done, T * q + t + 1)
                act.activation(y_hi[:, par, t, :], y[:, par, t, :], ACT.Copy).then_inc(yhi_done, 1)

            def yT_high(q, t):
                act.wait_ge(yT_done, T * q + t + 1)
                act.activation(yT_hi[:, :, t * P:(t + 1) * P], yt_ps[t % 2].rearrange("p (k c) -> p k c", k=KD),
                               ACT.Copy).then_inc(yT_hi_done, 1)

            def norm_context(b, t):
                act.wait_ge(c_off, T * b + t + 1)
                act.activation(ctxn[:, t % 2, :], c_ps[t % 2][:, :], ACT.Identity, bias=off_c[:, t:t + 1],
                               scale=rstd_c[:, t:t + 1]).then_inc(ctxn_done, 1)

            def norm_z(q, h, par, t):
                act.wait_ge(z_off, T * q + t + 1)
                if not isinstance(q, int) or q >= 2:
                    act.wait_ge(scat[par][t], 32 * h)
                act.activation(z[:, par, t, 0:D], x1[:, t % 2, :], ACT.Identity, bias=off_z[:, t:t + 1],
                               scale=rstd_z[:, t:t + 1]).then_inc(z_done, 1)

            def zT_high(q, t, i=0):
                act.wait_ge(ztr_done, T * q + t + 1)
                act.activation(zT_hi[:, i, :], zt_ps[i], ACT.Copy).then_inc(zT_hi_done, 1)

            def copy_logits(q, t, i=0):
                act.wait_ge(gate_done, T * q + t + 1)
                if t == 0 and not is_first(q):
                    act.wait_ge(chosen_done, q)
                act.activation(lg_parts[:, t, :, :].rearrange("p h e -> p (h e)"), zt_ps[i][:, 0:2 * E], ACT.Copy,
                               scale=1.0 / WSCALE).then_inc(lg_done, 1)

            def p_high(b, j):
                act.wait_ge(inv_done, T * b + j + 1)
                act.activation(p_hi[:, j, :], p32[:, j % 3, :], ACT.Copy, scale=pinv[:, j:j + 1]).then_inc(phi_done, 1)

            def weights_high(i):
                e, dst = i // 2, (w2_hi if i % 2 else w1_hi)
                act.wait_ge(w_in[i % 4], 16 * (i // 4 + 1))
                act.activation(dst[:, e, :], stage[:, i % 4, :], ACT.Copy, scale=WSCALE).then_inc(whi_done, 1)

            def router_exp(n, lo=0, hi=T):
                act.wait_ge(lgd_done, n + 1)
                act.activation(lge[:, lo:hi, :], lgd[:, lo:hi, :], ACT.Exp).then_inc(lge_done, 1)

            AHEAD = 6

            def batch(b, h, par):
                before_h = h if par else h - 1
                for j in range(T):
                    n = T * b + j
                    if not is_first(b) and j < 3:
                        zT_high(b - 1, T - 3 + j)
                    act.wait_ge(max_done, n + 1)
                    sp_ = s_ps[j % 2]
                    if j < T - 1:
                        act.activation(above[j][:, :], sp_[:, (j + 1) * P:S], ACT.Copy).then_inc(above_done, 1)
                    if j >= 3:
                        act.wait_ge(plo_done, n - 2)
                    act.activation(p32[:, j % 3, :], sp_[:, :], ACT.Exp, bias=neg_max[:, j:j + 1],
                                   accum_out=psum_row[:, j:j + 1]).then_inc(exp_done, 1)
                    if j:
                        if j == 1 and not is_first(b):
                            act.wait_ge(pv_done, T * b)
                        p_high(b, j - 1)
                    if not is_first(b) and j == 0:
                        norm_z(b - 1, before_h, 1 - par, T - 1)
                    if not is_first(b) and j < 3:
                        copy_logits(b - 1, T - 3 + j)
                p_high(b, T - 1)
                if not is_last(b):
                    for t in range(AHEAD):
                        norm_x(b + 1, 1 - par, t)
                for t in range(1, T + 1):
                    if t >= 4:
                        zT_high(b, t - 4)
                    if not is_last(b):
                        for u in Y_AHEAD.get(t, ()):
                            yT_high(b + 1, u)
                    if is_last(b):
                        for i in split_under(t):
                            weights_high(i)
                        if t == T:
                            zT_high(b, T - 3, 1)
                    soon = is_last(b) and t == T - 1
                    if soon:
                        copy_logits(b, t - 4)
                    norm_context(b, t - 1)
                    if t == 1 and not is_first(b):
                        router_exp(b - 1)
                    if t >= 4 and not soon:
                        copy_logits(b, t - 4)
                    if t == T and is_last(b):
                        copy_logits(b, T - 3, 1)
                    if t >= 2:
                        norm_z(b, h, par, t - 2)
                    if not is_last(b):
                        if t - 1 + AHEAD < T:
                            norm_x(b + 1, 1 - par, t - 1 + AHEAD)
                        y_high(b + 1, 1 - par, t - 1)
                    elif t == T - 1:
                        router_exp(B - 1, 0, CUT)

            act.wait_ge(const_dma, 16)
            act.activation(gate_hl[:, :, 0, :], gate[:, :, :], ACT.Copy, scale=WSCALE).then_inc(gate_hi_done, 1)
            for t in range(3):
                norm_x(0, 0, t)
            for t in range(T):
                yT_high(0, t)
                if t + 3 < T:
                    norm_x(0, 0, t + 3)
            for t in range(T):
                y_high(0, 0, t)
            batches(act, batch)
            zT_high(B - 1, T - 2, 2)
            copy_logits(B - 1, T - 2, 2)
            weights_high(UNDER)
            norm_z(B - 1, B // 2 - 1, 1, T - 1)
            weights_high(UNDER + 1)
            zT_high(B - 1, T - 1, 0)
            copy_logits(B - 1, T - 1, 0)
            router_exp(B, CUT, T)
            for i in range(UNDER + 2, STAGES):
                weights_high(i)
            act.wait_ge(consts, NCONST)
            act.activation(warm[:, :], pow_exp[0:1, 0:1], ACT.Gelu).then_inc(warm_done, 1)

            act.wait_ge(b_in, 32)
            act.wait_ge(tab_done, 1)

            def slots_high(g, par):
                for c in range(2):
                    act.wait_ge(tr_done, 2 * g + c + 1)
                    if c == 0 and (not isinstance(g, int) or g >= 2):
                        act.wait_ge(h_done, g - 1)
                    act.activation(s_hi[:, par, c * HALF:(c + 1) * HALF], tr_ps[c][:, :], ACT.Copy).then_inc(shi_done, 1)

            def gelu(g, par):
                e2 = act.value_load(tile_e[0:1, bass.ds(g, 1)], min_val=0, max_val=E - 1) * MH
                act.wait_ge(h_done, g + 1)
                if not isinstance(g, int) or g >= 2:
                    act.wait_ge(hlo_done, g - 1)
                for m in range(MH):
                    act.activation(h32[:, par, m * SLOT:(m + 1) * SLOT], h_ps[par][:, m * SLOT:(m + 1) * SLOT],
                                   ACT.Gelu, bias=b1_col[:, bass.ds(e2 + m, 1)], scale=1.0 / WSCALE).then_inc(gelu_done, 1)

            def step(s, par=None):
                par = s % 2 if par is None else par
                if not isinstance(s, int) or s + 1 < G:
                    slots_high(s + 1, 1 - par)
                if not isinstance(s, int) or s < G:
                    gelu(s, par)
            slots_high(0, 0)
            expert_steps(act, step)

            def final_norm(q, par):
                act.wait_ge(f_off, q + 1)
                for t in range(QT):
                    act.activation(fin_a[:, par, t, :], fin_a[:, par, t, :], ACT.Identity, bias=off_f[:, par, t:t + 1],
                                   scale=mul_f[:, par, t:t + 1]).then_inc(f_norm, 1)

            def store_final(q, par):
                act.wait_ge(f_sum, q + 1)
                act.dma_start(out_v[:, bass.ds(QT * q, QT), :], fin_x[:, par, :, :]).then_inc(fin_out[par], 16)

            def final(i, par, end=False):
                q = FB * i + par
                if not end:
                    final_norm(q + 1, (par + 1) % FB)
                store_final(q, par)
            final_norm(0, 0)
            for par in range(FB):
                final(0, par)
            for par in range(FB):
                final(1, par, par == FB - 1)

        @block.vector
        def _(dve):
            dve.memset(ones[:, :], 1.0).then_inc(dve_consts, 1)
            dve.memset(v_ones[:, :], 1.0).then_inc(dve_consts, 1)
            dve.memset(v_next[:, :], 1.0).then_inc(dve_consts, 1)
            dve.memset(v_base[:, V:V + 1], float(E * CAP)).then_inc(dve_consts, 1)
            dve.wait_ge(dve_consts, 4)
            dve.memset(v_next[:, E - 1:E], float(1 - E)).then_inc(dve_consts, 1)
            dve.memset(v_next[:, V - 1:V], 0.0).then_inc(dve_consts, 1)

            def stats(src, st, mv, var, off, rstd, eps, done, i, n):
                stat_s, mv_s, var_s = done
                dve.bn_stats(st[:, i, :], src).then_inc(stat_s, 1)
                dve.wait_ge(stat_s, n + 1)
                dve.nop(nofuse=True)
                dve.bn_aggr(mv[:, i, :], st[:, i, :]).then_inc(mv_s, 1)
                dve.wait_ge(mv_s, n + 1)
                dve.tensor_scalar(var[:, i:i + 1], mv[:, i, 1:2], eps, None, ALU.add).then_inc(var_s, 1)

            def offset(mv, rstd, off, rstd_s, off_s, i, n):
                dve.wait_ge(rstd_s, n + 1)
                dve.scalar_tensor_tensor(off[:, i:i + 1], mv[:, i, 0:1], -1.0, rstd[:, i:i + 1],
                                         ALU.mult, ALU.mult).then_inc(off_s, 1)

            def ln1_stat(q, h, par, tiles):
                if not is_first(q):
                    dve.wait_ge(x_in[par], 16 * (h + par))
                for t in tiles:
                    if is_first(q) and t % 2 == 0:
                        dve.wait_ge(x_first[t // 2], 16)
                        dve.nop(nofuse=True)
                    last = dve.bn_stats(st_x[:, t, :], y[:, par, t, :])
                if T - 1 in tiles:
                    last.then_inc(ln1_stats, 1)

            def ln1_moments(q):
                dve.wait_ge(ln1_stats, q + 1)
                dve.nop(nofuse=True)
                for t in range(T):
                    last = dve.bn_aggr(mv_x[:, t, :], st_x[:, t, :])
                last.then_inc(ln1_mv, 1)
                dve.wait_ge(ln1_mv, q + 1)
                dve.tensor_scalar(var_x[:, :], mv_x[:, :, 1], EPS, None, ALU.add).then_inc(ln1_var, 1)

            def ln1_offset(q):
                dve.wait_ge(ln1_rstd, q + 1)
                dve.scalar_tensor_tensor(off_x[:, :], mv_x[:, :, 0], -1.0, rstd_x[:, :], ALU.mult, ALU.mult).then_inc(ln1_off, 1)

            def yT_low(q, t):
                dve.wait_ge(yT_hi_done, T * q + t + 1)
                cols = slice(t * P, (t + 1) * P)
                dve.tensor_tensor(yT_lo[:, :, cols], yt_ps[t % 2].rearrange("p (k c) -> p k c", k=KD),
                                  yT_hi[:, :, cols], ALU.subtract).then_inc(yT_lo_done, 1)

            def zT_low(q, t, i=0):
                dve.wait_ge(zT_hi_done, T * q + t + 1)
                dve.tensor_tensor(zT_lo[:, i, :], zt_ps[i], zT_hi[:, i, :], ALU.subtract).then_inc(zT_lo_done, 1)

            def c_step(m, t):
                dve.wait_ge(pv_done, m + 1)
                stats(c_ps[t % 2][:, :], st_c, mv_c, var_c, off_c, rstd_c, EPS * PSCALE * PSCALE,
                      (c_stats, c_mv, c_var), t, m)

            def z_step(m, t):
                dve.wait_ge(x1_done, m + 1)
                stats(x1[:, t % 2, :], st_z, mv_z, var_z, off_z, rstd_z, EPS, (z_stats, z_mv, z_var), t, m)

            def row_sum(b, j):
                n = T * b + j
                dve.wait_ge(exp_done, n + 1)
                dve.tensor_scalar(psum_sc[:, j:j + 1], psum_row[:, j:j + 1], 1.0 / PSCALE, None, ALU.mult).then_inc(sum_done, 1)
                dve.wait_ge(sum_done, n + 1)
                dve.reciprocal(pinv[:, j:j + 1], psum_sc[:, j:j + 1]).then_inc(inv_done, 1)

            def p_low(b, j):
                dve.wait_ge(phi_done, T * b + j + 1)
                dve.scalar_tensor_tensor(p_lo[:, j, :], p32[:, j % 3, :], pinv[:, j:j + 1], p_hi[:, j, :],
                                         ALU.mult, ALU.subtract).then_inc(plo_done, 1)

            def weights_low(i):
                e, lo, hi = i // 2, (w2_lo if i % 2 else w1_lo), (w2_hi if i % 2 else w1_hi)
                dve.wait_ge(whi_done, i + 1)
                dve.scalar_tensor_tensor(lo[:, e, :], stage[:, i % 4, :], WSCALE, hi[:, e, :],
                                         ALU.mult, ALU.subtract).then_inc(wlo_done, 1)

            def wide(col):
                return col.unsqueeze(2).broadcast_to([P, col.shape[1], E])

            def across(row, tiles):
                return row.unsqueeze(1).broadcast_to([P, tiles, E])

            def router(q, par, part, n=None, lo=0, hi=T):
                n = q if n is None else n
                base = ROUTE * n
                tiles = slice(lo, hi)
                W = (hi - lo) * E
                flat = "p t e -> p (t e)"
                if part == 0:
                    dve.wait_ge(lg_done, T * q + hi)
                    dve.tensor_tensor(lg[:, tiles, :], lg_parts[:, tiles, 0, :], lg_parts[:, tiles, 1, :], ALU.add).then_inc(route, 1)
                    dve.wait_ge(route, base + 1)
                    dve.tensor_reduce(top[:, 0, tiles], lg[:, tiles, :], X, ALU.max).then_inc(route, 1)
                    dve.wait_ge(route, base + 2)
                    dve.tensor_tensor(lgd[:, tiles, :], lg[:, tiles, :], wide(top[:, 0, tiles]), ALU.subtract).then_inc(lgd_done, 1)
                    dve.tensor_tensor(eq[:, tiles, :], lg[:, tiles, :], wide(top[:, 0, tiles]), ALU.is_equal).then_inc(route, 1)
                    dve.wait_ge(route, base + 3)
                    dve.tensor_tensor(gnum[:, tiles, :], eq[:, tiles, :], across(rev[:, :], hi - lo), ALU.mult).then_inc(route, 1)
                    dve.wait_ge(route, base + 4)
                    dve.tensor_reduce(top[:, 1, tiles], gnum[:, tiles, :], X, ALU.max).then_inc(route, 1)
                    dve.wait_ge(route, base + 5)
                    dve.tensor_tensor(first[:, tiles, :], across(rev[:, :], hi - lo), wide(top[:, 1, tiles]), ALU.is_equal).then_inc(route, 1)
                    dve.wait_ge(route, base + 6)
                    dve.scalar_tensor_tensor(lg2[:, tiles, :].rearrange(flat), first[:, tiles, :].rearrange(flat), FAR,
                                             lg[:, tiles, :].rearrange(flat), ALU.mult, ALU.add).then_inc(route, 1)
                if part == 1:
                    dve.wait_ge(route, base + 7)
                    dve.tensor_reduce(top[:, 2, tiles], lg2[:, tiles, :], X, ALU.max).then_inc(route, 1)
                    dve.wait_ge(route, base + 8)
                    dve.tensor_tensor(eq[:, tiles, :], lg2[:, tiles, :], wide(top[:, 2, tiles]), ALU.is_equal).then_inc(route, 1)
                    dve.wait_ge(route, base + 9)
                    dve.tensor_tensor(gnum[:, tiles, :], eq[:, tiles, :], across(rev[:, :], hi - lo), ALU.mult).then_inc(route, 1)
                    dve.wait_ge(route, base + 10)
                    dve.tensor_reduce(top[:, 3, tiles], gnum[:, tiles, :], X, ALU.max).then_inc(route, 1)
                    dve.wait_ge(route, base + 11)
                    dve.tensor_tensor(second[:, tiles, :], across(rev[:, :], hi - lo), wide(top[:, 3, tiles]), ALU.is_equal).then_inc(route, 1)
                    dve.wait_ge(route, base + 12)
                    dve.tensor_tensor(chosen[:, tiles, :], first[:, tiles, :], second[:, tiles, :], ALU.add).then_inc(chosen_done, 1)
                if part == 2:
                    dve.wait_ge(lge_done, n + 1)
                    dve.wait_ge(chosen_done, n + 1)
                    dve.tensor_tensor(gnum[:, tiles, :], chosen[:, tiles, :], lge[:, tiles, :], ALU.mult).then_inc(gate_sums, 1)
                    dve.tensor_reduce(top[:, 4, tiles], lge[:, tiles, :], X, ALU.add).then_inc(gate_sums, 1)
                    dve.wait_ge(gate_sums, 5 * n + 2)
                    dve.tensor_reduce(top[:, 5, tiles], gnum[:, tiles, :], X, ALU.add).then_inc(gate_sums, 1)
                    dve.reciprocal(top[:, 0, tiles], top[:, 4, tiles]).then_inc(gate_sums, 1)
                    dve.wait_ge(gate_sums, 5 * n + 4)
                    dve.tensor_tensor(tok_w[:, bass.ds(T * q + lo, hi - lo)], top[:, 5, tiles], top[:, 0, tiles], ALU.mult).then_inc(gate_sums, 1)
                if part == 3:
                    dve.wait_ge(rank_done, n + 1)
                    dve.tensor_tensor(place[:, tiles, :], z_ps[:, 0:W].rearrange("p (t e) -> p t e", e=E),
                                      across(carry[:, :], hi - lo), ALU.add).then_inc(route, 1)
                    dve.wait_ge(route, base + 13)
                    dve.tensor_tensor(carry[:, :], carry[:, :], z_ps[:, W:W + E], ALU.add).then_inc(route, 1)
                    if lo == 0:
                        dve.tensor_scalar(token[:, :], token[:, :], float(S), None, ALU.add).then_inc(token_done, 1)
                    dve.tensor_tensor(place1[:, tiles, :], place[:, tiles, :], first[:, tiles, :], ALU.mult)
                    dve.tensor_tensor(place2[:, tiles, :], place[:, tiles, :], second[:, tiles, :], ALU.mult).then_inc(route, 1)
                    dve.wait_ge(route, base + 15)
                    dve.tensor_reduce(slot_f[:, tiles, 0], place1[:, tiles, :], X, ALU.add)
                    dve.tensor_reduce(slot_f[:, tiles, 1], place2[:, tiles, :], X, ALU.add).then_inc(slot_f_done, 1)
                    dve.wait_ge(token_done, q + 1)
                    dve.tensor_copy(z[:, par, tiles, D:D + 1].bitcast(U32), token[:, tiles].unsqueeze(2))
                    dve.wait_ge(slot_f_done, n + 1)
                    dve.tensor_copy(slot[:, par, tiles, :], slot_f[:, tiles, :]).then_inc(slot_done, 1)

            def z_offset(b, t):
                offset(mv_z, rstd_z, off_z, z_rstd, z_off, t, T * b + t)

            def batch(b, h, par):
                next_h = h + par
                for j in range(T):
                    n = T * b + j
                    dve.wait_ge(s_done, n + 1)
                    dve.tensor_reduce(neg_max[:, j:j + 1], s_ps[j % 2][:, :], X, ALU.max, negate=True).then_inc(max_done, 1)
                    if not is_first(b) and j < 3:
                        zT_low(b - 1, T - 3 + j)
                    if not is_first(b) and j == 0:
                        z_step(T * b - 1, T - 1)
                        z_offset(b - 1, T - 1)
                    if j:
                        row_sum(b, j - 1)
                    if j >= 2:
                        p_low(b, j - 2)
                    if not is_last(b):
                        if j < 3:
                            ln1_stat(b + 1, next_h, 1 - par, range(3 * j, min(3 * j + 3, T)))
                        if j == 3:
                            ln1_moments(b + 1)
                        if j == 5:
                            ln1_offset(b + 1)
                row_sum(b, T - 1)
                p_low(b, T - 2)
                p_low(b, T - 1)
                for t in range(1, T + 1):
                    if is_last(b) and t == T:
                        break
                    c_step(T * b + t - 1, t - 1)
                    if t == 2 and not is_first(b):
                        router(b - 1, 1 - par, 1)
                    if t >= 4:
                        zT_low(b, t - 4)
                    if t < 3:
                        offset(mv_c, rstd_c, off_c, c_rstd, c_off, t - 1, T * b + t - 1)
                    if t >= 2:
                        z_step(T * b + t - 2, t - 2)
                    if not is_last(b):
                        for u in Y_AHEAD.get(t, ()):
                            yT_low(b + 1, u)
                    if t >= 3:
                        offset(mv_c, rstd_c, off_c, c_rstd, c_off, t - 1, T * b + t - 1)
                    if t >= 2:
                        z_offset(b, t - 2)
                    if not is_first(b):
                        for part in {1: (0,), 2: (2,), 3: (3,)}.get(t, ()):
                            router(b - 1, 1 - par, part)
                    if is_last(b):
                        for i in split_under(t):
                            weights_low(i)
                        if t == T - 1:
                            router(b, par, 0, B - 1, 0, CUT)

            ln1_stat(0, 0, 0, range(T))
            ln1_moments(0)
            ln1_offset(0)
            dve.wait_ge(gate_hi_done, 1)
            dve.scalar_tensor_tensor(gate_hl[:, :, 1, :], gate[:, :, :], WSCALE, gate_hl[:, :, 0, :],
                                     ALU.mult, ALU.subtract).then_inc(gate_lo_done, 1)
            for t in range(T):
                yT_low(0, t)
            dve.wait_ge(consts, NCONST)
            batches(dve, batch)
            c_step(NT - 1, T - 1)
            z_step(NT - 2, T - 2)
            offset(mv_c, rstd_c, off_c, c_rstd, c_off, T - 1, NT - 1)
            zT_low(B - 1, T - 4)
            z_offset(B - 1, T - 2)
            router(B - 1, 1, 1, B - 1, 0, CUT)
            zT_low(B - 1, T - 3, 1)
            z_step(NT - 1, T - 1)
            router(B - 1, 1, 3, B - 1, 0, CUT)
            z_offset(B - 1, T - 1)
            zT_low(B - 1, T - 2, 2)
            router(B - 1, 1, 2, B - 1, 0, CUT)
            weights_low(UNDER)
            zT_low(B - 1, T - 1, 0)
            for part in (0, 1, 3):
                router(B - 1, 1, part, B, CUT, T)

            dve.wait_ge(slot_done, B + 1)
            dve.wait_ge(dve_consts, 6)
            dve.tensor_copy(pad_row[:, :], carry[0:1, :]).then_inc(pads_at, 1)
            for i in range(UNDER + 1, UNDER + 3):
                weights_low(i)
            dve.tensor_scalar(v_base[:, 0:E], rev[0:1, :], -float(CAP), float(E * CAP), ALU.mult, ALU.add).then_inc(tab_step, 1)
            dve.wait_ge(tab_step, 2)
            dve.tensor_tensor(lens[:, :], carry[0:1, :], v_base[:, 0:E], ALU.subtract).then_inc(tab_step, 1)
            dve.wait_ge(tab_step, 3)
            dve.tensor_scalar(halves_i[:, 0, :], lens[:, :], float(0), None, ALU.add)
            dve.tensor_scalar(halves_i[:, 1, :], lens[:, :], float(SLOT - 1), None, ALU.add).then_inc(tab_step, 1)
            dve.wait_ge(tab_step, 4)
            dve.tensor_scalar(halves_i[:, :, :], halves_i[:, :, :], SLOT.bit_length() - 1, None, ALU.logical_shift_right).then_inc(tab_step, 1)
            dve.wait_ge(tab_step, 5)
            dve.tensor_copy(halves[:, :, :], halves_i[:, :, :]).then_inc(tab_step, 1)
            dve.wait_ge(tab_step, 6)
            dve.tensor_copy(v_tiles[:, 0:E], halves[:, 0, :])
            dve.tensor_tensor(v_tiles[:, E:V], halves[:, 1, :], halves[:, 0, :], ALU.subtract).then_inc(tab_step, 1)
            dve.wait_ge(tab_step, 7)
            dve.tensor_tensor_scan(v_end[:, :], v_ones[:, :], v_tiles[:, :], 0.0, ALU.mult, ALU.add).then_inc(tab_step, 1)
            dve.wait_ge(tab_step, 8)
            dve.scalar_tensor_tensor(v_base[:, E:V], halves[:, 0, :], float(SLOT), v_base[:, 0:E], ALU.mult, ALU.add).then_inc(tab_step, 1)
            dve.wait_ge(tab_step, 9)
            dve.tensor_tensor(v_step[:, :], v_base[:, 1:V + 1], v_base[:, 0:V], ALU.subtract).then_inc(tab_step, 1)
            dve.wait_ge(tab_step, 10)
            dve.scalar_tensor_tensor(v_jump[:, :], v_tiles[:, :], -float(SLOT), v_step[:, :], ALU.mult, ALU.add).then_inc(tab_step, 1)
            dve.wait_ge(tab_step, 11)

            def tiles_by(v):
                return v[:, :].unsqueeze(1).broadcast_to([1, G, V])
            dve.tensor_tensor(passed[:, :, :], tab_g[:, :].unsqueeze(2).broadcast_to([1, G, V]),
                              tiles_by(v_end), ALU.is_ge).then_inc(tab_step, 1)
            dve.wait_ge(tab_step, 12)
            dve.tensor_tensor(passed_e[:, :, :], passed[:, :, :], tiles_by(v_next), ALU.mult)
            dve.tensor_tensor(passed_row[:, :, :], passed[:, :, :], tiles_by(v_jump), ALU.mult).then_inc(tab_step, 1)
            dve.wait_ge(tab_step, 13)
            dve.tensor_reduce(tab_e[:, :], passed_e[:, :, :], X, ALU.add)
            dve.tensor_reduce(tab_r[:, :], passed_row[:, :, :], X, ALU.add).then_inc(tab_step, 1)
            dve.wait_ge(tab_step, 14)
            dve.scalar_tensor_tensor(tile_row[:, :], tab_g[:, :], float(SLOT), tab_r[:, :], ALU.mult, ALU.add)
            dve.tensor_copy(tile_e[:, :], tab_e[:, :]).then_inc(tab_done, 1)

            for i in range(UNDER + 3, STAGES):
                weights_low(i)
            router(B - 1, 1, 2, B, CUT, T)
            dve.wait_ge(b_in, 32)
            dve.wait_ge(tab_done, 1)

            def slots_low(g, par):
                for c in range(2):
                    dve.wait_ge(shi_done, 2 * g + c + 1)
                    cols = slice(c * HALF, (c + 1) * HALF)
                    dve.tensor_tensor(s_lo[:, par, cols], tr_ps[c][:, :], s_hi[:, par, cols], ALU.subtract).then_inc(slo_done, 1)
                dve.tensor_copy(who_all[:, bass.ds(SH * g, SH)].unsqueeze(2), zin[:, par, :, D:D + 1].bitcast(U32)).then_inc(who_in, 1)

            def split_hidden(g, par):
                dve.wait_ge(gelu_done, MH * (g + 1))
                if not isinstance(g, int) or g >= 2:
                    dve.wait_ge(ye_done, SH * (g - 1))
                dve.tensor_copy(h_hi[:, par, :], h32[:, par, :]).then_inc(hhi_done, 1)
                dve.wait_ge(hhi_done, g + 1)
                dve.tensor_tensor(h_lo[:, par, :], h32[:, par, :], h_hi[:, par, :], ALU.subtract).then_inc(hlo_done, 1)

            def expert_out(g, par):
                at = dve.value_load(tile_e[0:1, bass.ds(g, 1)], min_val=0, max_val=E - 1) * D
                if not isinstance(g, int) or g >= 2:
                    dve.wait_ge(added, 16 * SH * (g - 1))
                dve.wait_ge(who_in, g + 1)
                dve.tensor_copy(who[:, par, :], who_all[:, bass.ds(SH * g, SH)]).then_inc(who_done, 1)
                for s in range(SH):
                    dve.wait_ge(ye_done, SH * g + s + 1)
                    dve.scalar_tensor_tensor(yo[:, par, s, :], y_ps[par][s][:, :], 1.0 / WSCALE,
                                             b2_all[:, bass.ds(at, D)], ALU.mult, ALU.add).then_inc(yo_done, 1)

            def step(s, par=None):
                par = s % 2 if par is None else par
                if not isinstance(s, int) or s + 1 < G:
                    slots_low(s + 1, 1 - par)
                if not isinstance(s, int) or s < G:
                    split_hidden(s, par)
                if not isinstance(s, int) or s >= 1:
                    expert_out(s - 1, 1 - par)
            slots_low(0, 0)
            expert_steps(dve, step)

            def final_stats(q, i, par):
                w = tok_w[:, bass.ds(QT * q, QT)]
                dve.wait_ge(fin_a_in[par], 16 * i + 16)
                for t in range(QT):
                    last = dve.bn_stats(st_f[:, par, t, :], fin_a[:, par, t, :])
                last.then_inc(f_stats, 1)
                dve.tensor_tensor(w_sq[:, par, :], w, w, ALU.mult).then_inc(f_sq, 1)
                dve.wait_ge(f_stats, q + 1)
                dve.nop(nofuse=True)
                for t in range(QT):
                    last = dve.bn_aggr(mv_f[:, par, t, :], st_f[:, par, t, :])
                last.then_inc(f_mv, 1)
                dve.wait_ge(f_mv, q + 1)
                dve.wait_ge(f_sq, q + 1)
                dve.tensor_tensor(var_f[:, par, :], mv_f[:, par, :, 1], w_sq[:, par, :], ALU.mult).then_inc(f_var, 1)
                dve.wait_ge(f_var, q + 1)
                dve.tensor_scalar(ve_f[:, par, :], var_f[:, par, :], EPS, None, ALU.add).then_inc(f_ve, 1)

            def final_offset(q, par):
                dve.wait_ge(f_rstd, q + 1)
                dve.tensor_tensor(mul_f[:, par, :], rstd_f[:, par, :], tok_w[:, bass.ds(QT * q, QT)], ALU.mult).then_inc(f_mul, 1)
                dve.wait_ge(f_mul, q + 1)
                dve.scalar_tensor_tensor(off_f[:, par, :], mv_f[:, par, :, 0], -1.0, mul_f[:, par, :],
                                         ALU.mult, ALU.mult).then_inc(f_off, 1)

            def final(i, par, end=False):
                q = FB * i + par
                if not end:
                    final_stats(q + 1, i + (par + 1) // FB, (par + 1) % FB)
                final_offset(q, par)
            final_stats(0, 0, 0)
            for par in range(FB):
                final(0, par)
            for par in range(FB):
                final(1, par, par == FB - 1)

        @block.tensor
        def _(pe):
            def transpose_y(q, par, t):
                n = T * q + t
                pe.wait_ge(y_done, n + 1)
                if t % 2 and not is_first(q):
                    pe.wait_ge(exp_done, T * q)
                if not isinstance(n, int) or n >= 2:
                    pe.wait_ge(yT_lo_done, n - 1)
                for k in range(KD):
                    last = pe.transpose(yt_ps[t % 2][:, k * P:(k + 1) * P], y[:, par, t, k * P:(k + 1) * P], ident[:, :])
                last.then_inc(yT_done, 1)

            def scores(b, j, between, fill):
                n = T * b + j
                if j == 0:
                    pe.wait_ge(yT_lo_done, T * (b + 1))
                if not isinstance(n, int) or n >= 2:
                    pe.wait_ge(exp_done, n - 1)
                row = s_ps[j % 2]
                mine = slice(j * P, (j + 1) * P)
                chunks = [(max(j * P, c * HALF), (c + 1) * HALF) for c in range(2) if (c + 1) * HALF > j * P]
                for c, (lo, hi) in enumerate(chunks):
                    if c == len(chunks) - 1:
                        between()
                    for k in range(KD):
                        for i, (l, r) in enumerate(((yT_hi, yT_hi), (yT_hi, yT_lo), (yT_lo, yT_hi))):
                            last = pe.matmul(row[:, lo:hi], l[:, k, mine], r[:, k, lo:hi],
                                             start=(k == 0 and i == 0), stop=(k == KD - 1 and i == 2))
                fill()
                if j:
                    pe.wait_ge(above_done, (T - 1) * b + j)
                for i in range(j):
                    last = pe.transpose(row[:, i * P:(i + 1) * P],
                                        above[i][:, (j - i - 1) * P:(j - i) * P], ident[:, :])
                last.then_inc(s_done, 1)

            def context(b, par, t, js):
                m = T * b + t
                if 0 in js and (not isinstance(m, int) or m >= 2):
                    pe.wait_ge(ctxn_done, m - 1)
                rows = slice(t * P, (t + 1) * P)
                for j in js:
                    if t < 2:
                        pe.wait_ge(plo_done, T * b + j + 1)
                        pe.wait_ge(ylo_done, T * b + j + 1)
                    for i, (l, r) in enumerate(((p_hi, y_hi[:, par]), (p_hi, y_lo), (p_lo, y_hi[:, par]))):
                        last = pe.matmul(c_ps[t % 2][:, :], l[:, j, rows], r[:, j, :],
                                         start=(j == 0 and i == 0), stop=(j == T - 1 and i == 2))
                if T - 1 in js:
                    last.then_inc(pv_done, 1)

            def transpose_z(q, par, t, i=0):
                m = T * q + t
                pe.wait_ge(z_done, m + 1)
                if i == 0 and (not isinstance(m, int) or m):
                    pe.wait_ge(lg_done, m)
                if t == 0 and not is_first(q):
                    pe.wait_ge(slot_done, q)
                for k in range(KD):
                    last = pe.transpose(zt_ps[i][:, k * P:(k + 1) * P], z[:, par, t, k * P:(k + 1) * P], ident[:, :])
                last.then_inc(ztr_done, 1)

            def logits(q, t, i=0):
                pe.wait_ge(zT_lo_done, T * q + t + 1)
                for k in range(KD):
                    cols = slice(k * P, (k + 1) * P)
                    pe.matmul(zt_ps[i][:, 0:2 * E], zT_hi[:, i, cols], gate_hl[:, k, :, :].rearrange("p h e -> p (h e)"),
                              start=(k == 0), stop=False, skip_group_check=True)
                    last = pe.matmul(zt_ps[i][:, 0:E], zT_lo[:, i, cols], gate_hl[:, k, 0, :],
                                     start=False, stop=(k == KD - 1), skip_group_check=True)
                last.then_inc(gate_done, 1)

            def ranks(n, taken, lo=0, hi=T):
                pe.wait_ge(lg_done, taken)
                pe.wait_ge(chosen_done, n + 1)
                flat = chosen[:, lo:hi, :].rearrange("p t e -> p (t e)")
                tiles, W = hi - lo, (hi - lo) * E
                pe.matmul(z_ps[:, 0:W], before[:, :], flat, start=True, stop=False, skip_group_check=True)
                for s in range(1, tiles):
                    pe.matmul(z_ps[:, s * E:W], ones[:, :], flat[:, 0:W - s * E], start=False,
                              stop=(s == tiles - 1), skip_group_check=True)
                for s in range(tiles):
                    last = pe.matmul(z_ps[:, W:W + E], ones[:, :], flat[:, s * E:(s + 1) * E],
                                     start=(s == 0), stop=(s == tiles - 1), skip_group_check=True)
                last.then_inc(rank_done, 1)

            FILL = {5: (0,), 6: (1,), 7: (2, 3)}

            def batch(b, h, par):
                for j in range(T):
                    late = not is_first(b)
                    scores(b, j, (lambda: logits(b - 1, T - 4 + j)) if late and j < 3 else (lambda: None),
                           lambda: context(b, par, 0, FILL.get(j, ())))
                    if late and j < 3:
                        transpose_z(b - 1, 1 - par, T - 3 + j)
                    if late and j == 3:
                        logits(b - 1, T - 1)
                context(b, par, 0, [4])
                context(b, par, 1, range(5))
                context(b, par, 0, [5])
                context(b, par, 1, [5])
                context(b, par, 0, [6, 7])
                context(b, par, 1, [6, 7])
                for t in range(2, T):
                    if not is_last(b):
                        for u in Y_AHEAD[t]:
                            transpose_y(b + 1, 1 - par, u)
                    context(b, par, t, range(T // 2))
                    if t >= 4:
                        logits(b, t - 4)
                    context(b, par, t, range(T // 2, T))
                    if t == 2 and not is_first(b):
                        ranks(b - 1, T * b)
                    if t >= 3:
                        transpose_z(b, par, t - 3)

            pe.wait_ge(consts, NCONST)
            pe.wait_ge(dve_consts, 1)
            pe.wait_ge(gate_lo_done, 1)
            for t in range(T):
                transpose_y(0, 0, t)
            batches(pe, batch)
            pe.wait_ge(exp_done, NT)
            transpose_z(B - 1, 1, T - 3, 1)
            logits(B - 1, T - 4)
            logits(B - 1, T - 3, 1)
            ranks(B - 1, NT - 3, 0, CUT)
            transpose_z(B - 1, 1, T - 2, 2)
            logits(B - 1, T - 2, 2)
            pe.wait_ge(slot_done, B)
            transpose_z(B - 1, 1, T - 1, 0)
            logits(B - 1, T - 1, 0)
            ranks(B, NT, CUT, T)

            pe.wait_ge(tab_done, 1)
            pe.wait_ge(rank_done, B + 1)
            pe.wait_ge(slot_done, B + 1)

            def transpose_slots(g, par):
                odd = g % 2 if isinstance(g, int) else par
                count = (g // 2 + 1) * 16 if isinstance(g, int) else 8 * (g - par) + 16
                pe.wait_ge(zin_in[odd], count)
                for c in range(2):
                    if not isinstance(g, int) or g:
                        pe.wait_ge(slo_done, 2 * g - 1 + c)
                    for kk in range(2):
                        k = 2 * c + kk
                        for s in range(SH):
                            at = kk * SLOT + s * P
                            last = pe.transpose(tr_ps[c][:, at:at + P], zin[:, par, s, k * P:(k + 1) * P], ident[:, :])
                    last.then_inc(tr_done, 1)

            def up(g, par):
                e = pe.value_load(tile_e[0:1, bass.ds(g, 1)], min_val=0, max_val=E - 1)
                pe.wait_ge(slo_done, 2 * g + 2)
                if not isinstance(g, int) or g >= 2:
                    pe.wait_ge(gelu_done, MH * (g - 1))
                for m in range(MH):
                    for k in range(KD):
                        cols = slice(k * H + m * P, k * H + (m + 1) * P)
                        hi = w1_hi[:, bass.ds(e, 1), cols].rearrange("p e c -> p (e c)")
                        lo = w1_lo[:, bass.ds(e, 1), cols].rearrange("p e c -> p (e c)")
                        rows = slice(k * SLOT, (k + 1) * SLOT)
                        for i, (l, r) in enumerate(((hi, s_hi), (hi, s_lo), (lo, s_hi))):
                            last = pe.matmul(h_ps[par][:, m * SLOT:(m + 1) * SLOT], l, r[:, par, rows],
                                             start=(k == 0 and i == 0), stop=(k == KD - 1 and i == 2))
                last.then_inc(h_done, 1)

            def down(g, par):
                e = pe.value_load(tile_e[0:1, bass.ds(g, 1)], min_val=0, max_val=E - 1)
                pe.wait_ge(hlo_done, g + 1)
                for s in range(SH):
                    if not isinstance(g, int) or g >= 2:
                        pe.wait_ge(yo_done, SH * (g - 2) + s + 1)
                    for m in range(MH):
                        hi = w2_hi[:, bass.ds(e, 1), m * D:(m + 1) * D].rearrange("p e c -> p (e c)")
                        lo = w2_lo[:, bass.ds(e, 1), m * D:(m + 1) * D].rearrange("p e c -> p (e c)")
                        cols = slice(m * SLOT + s * P, m * SLOT + (s + 1) * P)
                        for i, (l, r) in enumerate(((h_hi, hi), (h_hi, lo), (h_lo, hi))):
                            last = pe.matmul(y_ps[par][s][:, :], l[:, par, cols], r,
                                             start=(m == 0 and i == 0), stop=(m == MH - 1 and i == 2))
                    last.then_inc(ye_done, 1)

            def step(s, par=None):
                par = s % 2 if par is None else par
                if not isinstance(s, int) or s + 1 < G:
                    transpose_slots(s + 1, 1 - par)
                if not isinstance(s, int) or s < G:
                    up(s, par)
                if not isinstance(s, int) or s >= 1:
                    down(s - 1, 1 - par)
            transpose_slots(0, 0)
            pe.wait_ge(wlo_done, STAGES)
            expert_steps(pe, step)


_INS = ["L0_attn_x", "L0_ffn_gate_w", "L0_ffn_w1", "L0_ffn_b1", "L0_ffn_w2", "L0_ffn_b2"]


def kernel(**inputs):
    import numpy as _np
    import concourse.bacc as _bacc
    from concourse.bass_utils import run_bass_kernel_spmd as _run

    nc = _bacc.Bacc("TRN2", target_bir_lowering=False, num_devices=1)
    arrays, args = {}, []
    for name in _INS:
        a = _np.ascontiguousarray(inputs[name])
        arrays[f"in_{name}"] = a
        args.append(nc.dram_tensor(f"in_{name}", a.shape, mybir.dt.from_np(a.dtype), kind="ExternalInput").ap())
    result = nc.dram_tensor("out_0", inputs["L0_attn_x"].shape, F32, kind="ExternalOutput").ap()
    attention_then_experts(nc, *args, result)
    r = _run(nc, [arrays], core_ids=[0])
    return r.results[0]["out_0"]
```
